# Optimizing a Trainium2 kernel written in Bass

```python
import numpy as np
import jax
import jax.numpy as jnp

def _softmax(x, axis=-1):
    return jax.nn.softmax(x, axis=axis)

def _gelu(x):
    return jax.nn.gelu(x, approximate=True)

def _silu(x):
    return jax.nn.silu(x)

def _sigmoid(x):
    return jax.nn.sigmoid(x)

def _layernorm(x, axis=-1, eps=1e-05):
    m = jnp.mean(x, axis=axis, keepdims=True)
    v = jnp.var(x, axis=axis, keepdims=True)
    return (x - m) / jnp.sqrt(v + eps)

def _scatter_add(tgt, idx, src, axis=0):
    return tgt.at[idx].add(src)

def _segment_sum(src, seg, n):
    return jax.ops.segment_sum(src, seg, n)
kernel_name = 'mk_cond_seq_d4_seqx_r4_28f910'

def setup_inputs(seed: int=0):
    np.random.seed(seed)
    _w = jnp.asarray

    def _rec_inputs():
        import jax
        import jax.numpy as jnp
        _rk = jax.random.key(seed)
        x = -1.528e-05 + 0.9999 * jax.random.normal(jax.random.fold_in(_rk, 1), (64, 64, 512), jnp.float32)
        _lenS = 64 - jax.random.randint(jax.random.fold_in(_rk, 7), (64,), 0, max(1, 64 // 4) + 1, jnp.int32)
        _lenS2 = 64 - jax.random.randint(jax.random.fold_in(_rk, 8), (64,), 0, max(1, 64 // 4) + 1, jnp.int32)
        itok_B_1_2 = jax.random.randint(jax.random.fold_in(_rk, 11), (64,), 1, 3, jnp.int32)
        itok_B_17_1546 = jax.random.randint(jax.random.fold_in(_rk, 13), (64,), 17, 1547, jnp.int32)
        return (x, itok_B_1_2, itok_B_17_1546, _lenS)
    x, itok_B_1_2, itok_B_17_1546, _lenS = _rec_inputs()

    def _L0_cond_setup():
        import jax, jax.numpy as jnp
        import numpy as np
        H = 512
        K = 256
        R = 3
        B = 8
        S = 512
        LN_EPS = 1e-05
        key = jax.random.key(seed)
        ks = jax.random.split(key, 8)
        sd_d = 1.0 / np.sqrt(H)
        sd_u = 1.0 / np.sqrt(K)
        return {'role': jax.random.randint(ks[0], (B,), 0, R), 'hidden_states': jax.random.normal(ks[1], (B, S, H), dtype=jnp.float32), 'W_down': jax.random.uniform(ks[2], (R, H, K), jnp.float32, -sd_d, sd_d), 'b_down': jax.random.uniform(ks[3], (R, K), jnp.float32, -sd_d, sd_d), 'W_up': jax.random.uniform(ks[4], (R, K, H), jnp.float32, -sd_u, sd_u), 'b_up': jax.random.uniform(ks[5], (R, H), jnp.float32, -sd_u, sd_u), 'gamma': jnp.ones((R, H), jnp.float32), 'beta': jnp.zeros((R, H), jnp.float32)}
    _L0_cond_all = _L0_cond_setup()
    _L0_cond_in = {k: v for k, v in _L0_cond_all.items() if k in ('W_down', 'b_down', 'W_up', 'b_up', 'gamma', 'beta')}
    del _L0_cond_all

    def _L1_cond_setup():
        import jax, jax.numpy as jnp
        import numpy as np
        B, T, V = (8, 128, 512)
        H = 4 * V
        key = jax.random.key(seed)
        ks = jax.random.split(key, 16)
        s = lambda n: 1.0 / np.sqrt(n)
        inp = {'x': jax.random.uniform(ks[0], (B, T, V), dtype=jnp.float32), 'lens': jax.random.randint(ks[1], (B,), 1, T, dtype=jnp.int64), 'target_codes': jax.random.randint(ks[2], (B,), 0, V, dtype=jnp.int64), 'Wq': jax.random.normal(ks[3], (V, V), jnp.float32) * s(V), 'Wk': jax.random.normal(ks[4], (V, V), jnp.float32) * s(V), 'Wv': jax.random.normal(ks[5], (V, V), jnp.float32) * s(V), 'Wp': jax.random.normal(ks[6], (V, V), jnp.float32) * s(V), 'bp': jnp.zeros((V,), jnp.float32), 'cW1': jax.random.normal(ks[7], (V, H), jnp.float32) * s(V), 'cb1': jnp.zeros((H,), jnp.float32), 'cW2': jax.random.normal(ks[8], (H, V), jnp.float32) * s(H), 'cb2': jnp.zeros((V,), jnp.float32), 'mW1': jax.random.normal(ks[9], (2 * V, H), jnp.float32) * s(2 * V), 'mb1': jnp.zeros((H,), jnp.float32), 'mW2': jax.random.normal(ks[10], (H, V), jnp.float32) * s(H), 'mb2': jnp.zeros((V,), jnp.float32)}
        return inp
    _L1_cond_all = _L1_cond_setup()
    _L1_cond_in = {k: v for k, v in _L1_cond_all.items() if k in ('Wq', 'Wk', 'Wv', 'Wp', 'bp', 'cW1', 'cb1', 'cW2', 'cb2', 'mW1', 'mb1', 'mW2', 'mb2')}
    del _L1_cond_all

    def _L2_cond_setup():
        import jax, jax.numpy as jnp
        import numpy as np
        H = 512
        K = 256
        R = 3
        B = 8
        S = 512
        LN_EPS = 1e-05
        key = jax.random.key(seed)
        ks = jax.random.split(key, 8)
        sd_d = 1.0 / np.sqrt(H)
        sd_u = 1.0 / np.sqrt(K)
        return {'role': jax.random.randint(ks[0], (B,), 0, R), 'hidden_states': jax.random.normal(ks[1], (B, S, H), dtype=jnp.float32), 'W_down': jax.random.uniform(ks[2], (R, H, K), jnp.float32, -sd_d, sd_d), 'b_down': jax.random.uniform(ks[3], (R, K), jnp.float32, -sd_d, sd_d), 'W_up': jax.random.uniform(ks[4], (R, K, H), jnp.float32, -sd_u, sd_u), 'b_up': jax.random.uniform(ks[5], (R, H), jnp.float32, -sd_u, sd_u), 'gamma': jnp.ones((R, H), jnp.float32), 'beta': jnp.zeros((R, H), jnp.float32)}
    _L2_cond_all = _L2_cond_setup()
    _L2_cond_in = {k: v for k, v in _L2_cond_all.items() if k in ('W_down', 'b_down', 'W_up', 'b_up', 'gamma', 'beta')}
    del _L2_cond_all

    def _L3_cond_setup():
        import jax, jax.numpy as jnp
        import numpy as np
        B, S, H = (8, 512, 512)
        BN = 256
        E = 3
        LN_EPS = 1e-05
        key = jax.random.key(seed)
        ks = jax.random.split(key, 8)
        stream = jax.random.randint(ks[0], (B,), 0, E, dtype=jnp.int32)
        hidden_states = jax.random.normal(ks[1], (B, S, H), dtype=jnp.float32)
        W_down = jax.random.normal(ks[2], (E, H, BN), dtype=jnp.float32) * 0.02
        b_down = jnp.zeros((E, BN), dtype=jnp.float32)
        W_up = jax.random.normal(ks[3], (E, BN, H), dtype=jnp.float32) * 0.02
        b_up = jnp.zeros((E, H), dtype=jnp.float32)
        ln_w = jnp.ones((E, H), dtype=jnp.float32)
        ln_b = jnp.zeros((E, H), dtype=jnp.float32)
        return {'stream': stream, 'hidden_states': hidden_states, 'W_down': W_down, 'b_down': b_down, 'W_up': W_up, 'b_up': b_up, 'ln_w': ln_w, 'ln_b': ln_b}
    _L3_cond_all = _L3_cond_setup()
    _L3_cond_in = {k: v for k, v in _L3_cond_all.items() if k in ('W_down', 'b_down', 'W_up', 'b_up', 'ln_w', 'ln_b')}
    del _L3_cond_all
    return {'x': x, 'itok_B_1_2': itok_B_1_2, 'itok_B_17_1546': itok_B_17_1546, '_lenS': _lenS, 'L0_cond_W_down': _L0_cond_in['W_down'], 'L0_cond_b_down': _L0_cond_in['b_down'], 'L0_cond_W_up': _L0_cond_in['W_up'], 'L0_cond_b_up': _L0_cond_in['b_up'], 'L0_cond_gamma': _L0_cond_in['gamma'], 'L0_cond_beta': _L0_cond_in['beta'], 'L1_cond_Wq': _L1_cond_in['Wq'], 'L1_cond_Wk': _L1_cond_in['Wk'], 'L1_cond_Wv': _L1_cond_in['Wv'], 'L1_cond_Wp': _L1_cond_in['Wp'], 'L1_cond_bp': _L1_cond_in['bp'], 'L1_cond_cW1': _L1_cond_in['cW1'], 'L1_cond_cb1': _L1_cond_in['cb1'], 'L1_cond_cW2': _L1_cond_in['cW2'], 'L1_cond_cb2': _L1_cond_in['cb2'], 'L1_cond_mW1': _L1_cond_in['mW1'], 'L1_cond_mb1': _L1_cond_in['mb1'], 'L1_cond_mW2': _L1_cond_in['mW2'], 'L1_cond_mb2': _L1_cond_in['mb2'], 'L2_cond_W_down': _L2_cond_in['W_down'], 'L2_cond_b_down': _L2_cond_in['b_down'], 'L2_cond_W_up': _L2_cond_in['W_up'], 'L2_cond_b_up': _L2_cond_in['b_up'], 'L2_cond_gamma': _L2_cond_in['gamma'], 'L2_cond_beta': _L2_cond_in['beta'], 'L3_cond_W_down': _L3_cond_in['W_down'], 'L3_cond_b_down': _L3_cond_in['b_down'], 'L3_cond_W_up': _L3_cond_in['W_up'], 'L3_cond_b_up': _L3_cond_in['b_up'], 'L3_cond_ln_w': _L3_cond_in['ln_w'], 'L3_cond_ln_b': _L3_cond_in['ln_b']}

def reference(x, itok_B_1_2, itok_B_17_1546, _lenS, L0_cond_W_down, L0_cond_b_down, L0_cond_W_up, L0_cond_b_up, L0_cond_gamma, L0_cond_beta, L1_cond_Wq, L1_cond_Wk, L1_cond_Wv, L1_cond_Wp, L1_cond_bp, L1_cond_cW1, L1_cond_cb1, L1_cond_cW2, L1_cond_cb2, L1_cond_mW1, L1_cond_mb1, L1_cond_mW2, L1_cond_mb2, L2_cond_W_down, L2_cond_b_down, L2_cond_W_up, L2_cond_b_up, L2_cond_gamma, L2_cond_beta, L3_cond_W_down, L3_cond_b_down, L3_cond_W_up, L3_cond_b_up, L3_cond_ln_w, L3_cond_ln_b):
    import jax
    import jax.numpy as jnp

    def _L0_cond_ref(role, hidden_states, W_down, b_down, W_up, b_up, gamma, beta):
        import jax, jax.numpy as jnp
        import numpy as np
        H = 512
        K = 256
        R = 3
        B = 8
        S = 512
        LN_EPS = 1e-05
        h = jnp.einsum('bsh,bhk->bsk', hidden_states, W_down[role]) + b_down[role][:, None, :]
        h = jax.nn.gelu(h, approximate=False)
        u = jnp.einsum('bsk,bkh->bsh', h, W_up[role]) + b_up[role][:, None, :]
        y = hidden_states + u
        mean = jnp.mean(y, axis=-1, keepdims=True)
        var = jnp.mean(jnp.square(y - mean), axis=-1, keepdims=True)
        yn = (y - mean) * jax.lax.rsqrt(var + LN_EPS)
        return yn * gamma[role][:, None, :] + beta[role][:, None, :]

    def _L1_cond_ref(x, lens, target_codes, Wq, Wk, Wv, Wp, bp, cW1, cb1, cW2, cb2, mW1, mb1, mW2, mb2):
        import jax, jax.numpy as jnp
        import numpy as np
        B, T, V = (8, 128, 512)
        H = 4 * V
        scale = V ** (-0.5)
        q = x @ Wq
        k = x @ Wk
        v = x @ Wv
        attn = jnp.einsum('btd,bTd->btT', q, k) * scale
        attn = jax.nn.softmax(attn, axis=-1)
        attn_out = jnp.einsum('btT,bTd->btd', attn, v) @ Wp + bp
        target_embed = jax.nn.one_hot(target_codes, V, dtype=x.dtype)[:, None, :]
        cms_out = jax.nn.gelu(attn_out @ cW1 + cb1, approximate=False) @ cW2 + cb2
        cms_out = cms_out + target_embed
        concat = jnp.concatenate([attn_out, cms_out], axis=-1)
        modifier = jax.nn.gelu(concat @ mW1 + mb1, approximate=False) @ mW2 + mb2
        out = jnp.clip(x + cms_out + modifier, 0.0, 1.0)
        return out

    def _L2_cond_ref(role, hidden_states, W_down, b_down, W_up, b_up, gamma, beta):
        import jax, jax.numpy as jnp
        import numpy as np
        H = 512
        K = 256
        R = 3
        B = 8
        S = 512
        LN_EPS = 1e-05
        h = jnp.einsum('bsh,bhk->bsk', hidden_states, W_down[role]) + b_down[role][:, None, :]
        h = jax.nn.gelu(h, approximate=False)
        u = jnp.einsum('bsk,bkh->bsh', h, W_up[role]) + b_up[role][:, None, :]
        y = hidden_states + u
        mean = jnp.mean(y, axis=-1, keepdims=True)
        var = jnp.mean(jnp.square(y - mean), axis=-1, keepdims=True)
        yn = (y - mean) * jax.lax.rsqrt(var + LN_EPS)
        return yn * gamma[role][:, None, :] + beta[role][:, None, :]

    def _L3_cond_ref(stream, hidden_states, W_down, b_down, W_up, b_up, ln_w, ln_b):
        import jax, jax.numpy as jnp
        import numpy as np
        B, S, H = (8, 512, 512)
        BN = 256
        E = 3
        LN_EPS = 1e-05
        Wd = W_down[stream]
        bd = b_down[stream]
        Wu = W_up[stream]
        bu = b_up[stream]
        g = ln_w[stream]
        b = ln_b[stream]
        residual = hidden_states
        h = jnp.einsum('bsh,bhk->bsk', hidden_states, Wd) + bd[:, None, :]
        h = jax.nn.gelu(h, approximate=False)
        h = jnp.einsum('bsk,bkh->bsh', h, Wu) + bu[:, None, :]
        h = residual + h
        mean = jnp.mean(h, axis=-1, keepdims=True)
        var = jnp.mean(jnp.square(h - mean), axis=-1, keepdims=True)
        h = (h - mean) * jax.lax.rsqrt(var + LN_EPS)
        return h * g[:, None, :] + b[:, None, :]
    x = _L0_cond_ref(itok_B_1_2, x, L0_cond_W_down, L0_cond_b_down, L0_cond_W_up, L0_cond_b_up, L0_cond_gamma, L0_cond_beta)
    x = _L1_cond_ref(x, _lenS, itok_B_17_1546, L1_cond_Wq, L1_cond_Wk, L1_cond_Wv, L1_cond_Wp, L1_cond_bp, L1_cond_cW1, L1_cond_cb1, L1_cond_cW2, L1_cond_cb2, L1_cond_mW1, L1_cond_mb1, L1_cond_mW2, L1_cond_mb2)
    x = _L2_cond_ref(itok_B_1_2, x, L2_cond_W_down, L2_cond_b_down, L2_cond_W_up, L2_cond_b_up, L2_cond_gamma, L2_cond_beta)
    x = _L3_cond_ref(itok_B_1_2, x, L3_cond_W_down, L3_cond_b_down, L3_cond_W_up, L3_cond_b_up, L3_cond_ln_w, L3_cond_ln_b)
    return x

_drawn_inputs = setup_inputs


def setup_inputs(seed=0):
    import zlib

    import numpy as np

    out = dict(_drawn_inputs(seed))
    spreads = {'L0_cond_gamma': (1.0, 0.2),
     'L0_cond_beta': (0.0, 0.1),
     'L1_cond_bp': (0.0, 0.1),
     'L1_cond_cb1': (0.0, 0.1),
     'L1_cond_cb2': (0.0, 0.1),
     'L1_cond_mb1': (0.0, 0.1),
     'L1_cond_mb2': (0.0, 0.1),
     'L2_cond_gamma': (1.0, 0.2),
     'L2_cond_beta': (0.0, 0.1),
     'L3_cond_b_down': (0.0, 0.452),
     'L3_cond_b_up': (0.0, 0.1),
     'L3_cond_ln_w': (1.0, 0.2),
     'L3_cond_ln_b': (0.0, 0.1)}
    factors = {'L0_cond_b_down': 4.112, 'L2_cond_b_down': 3.162}
    for name, (base, spread) in spreads.items():
        noise = np.random.default_rng([zlib.crc32(name.encode()), seed]).standard_normal(out[name].shape)
        drawn = base * np.exp(spread * noise) if base else spread * noise
        out[name] = jnp.asarray(drawn.astype(out[name].dtype))
    for name, factor in factors.items():
        out[name] = (out[name] * factor).astype(out[name].dtype)
    return out
```

```python
from contextlib import ExitStack

import concourse.bass as bass
from concourse import mybir

F32 = mybir.dt.float32
F32R = mybir.dt.float32r
I32 = mybir.dt.int32
ALU = mybir.AluOpType
ACT = mybir.ActivationFunctionType
AX = mybir.AxisListType.X

P = 128
NSEQ = 64
LEN = 64
D = 512
KD = D // P
BN = 256
KB = BN // P
ROLES = 3
HID = 4 * D
CH = HID // D
GS = 8
NG = NSEQ // GS + ROLES - 1
SLOTS = NG * GS
GT = GS * LEN // P
SROWS = LEN // GT
NROWS = NSEQ * SROWS
SB = 4
SBT = NSEQ * LEN // SB
TT = SBT // P
NH = SBT // 512
HT = TT // NH
SEQ_SB = NSEQ // SB
LN_EPS = 1e-5
SCALE = float(D) ** -0.5
WROW = KD * BN + KB * D + KB


def product(pe, out, terms):
    last = None
    for i, ((lh, ll), (rh, rl)) in enumerate(terms):
        pe.matmul(out, lh, rh, start=(i == 0), stop=False)
        pe.matmul(out, lh, rl, start=False, stop=False)
        last = pe.matmul(out, ll, rh, start=False, stop=(i == len(terms) - 1))
    return last


def route_and_fold(nc, consts, roles, codes, cb2, wqT, wkT, wvT, wp, fold_m, fold_v):
    tab_src, tab_dst, tab_row, target_bias, ident = consts
    with ExitStack() as ctx:
        def sb(name, shape, dt=F32):
            return ctx.enter_context(nc.sbuf_tensor(name, shape, dt))

        def sem(name):
            return ctx.enter_context(nc.semaphore(name))

        role_i = sb("role_i", [NSEQ, 1], I32)
        role_f = sb("role_f", [NSEQ, 1])
        role_c = sb("role_c", [NSEQ, 1])
        iota3 = sb("iota3", [NSEQ, ROLES])
        onehot = sb("onehot", [NSEQ, ROLES])
        before = sb("before", [NSEQ, NSEQ])
        ones = sb("ones", [NSEQ, NSEQ])
        up_i = sb("up_i", [NSEQ, ROLES], I32)
        up_r = sb("up_r", [NSEQ, ROLES], I32)
        base = sb("base", [NSEQ, ROLES])
        place = sb("place", [NSEQ, ROLES])
        placed = sb("placed", [NSEQ, ROLES])
        slot = sb("slot", [NSEQ, 1])
        iota_slot = sb("iota_slot", [NSEQ, SLOTS])
        at_slot = sb("at_slot", [NSEQ, SLOTS])
        off_slot = sb("off_slot", [NSEQ, SLOTS])
        at_row = sb("at_row", [NSEQ, SLOTS, SROWS])
        rows = sb("rows", [P, NG])
        slot_rows = sb("slot_rows", [P, NG])
        seq_off = sb("seq_off", [NSEQ, 1])
        iota_grp = sb("iota_grp", [1, NG])
        past1 = sb("past1", [1, NG])
        past2 = sb("past2", [1, NG])
        role_at = sb("role_at", [1, NG])
        codes_i = sb("codes_i", [P, NSEQ], I32)
        codes_f = sb("codes_f", [P, NSEQ])
        feat = sb("feat", [P, KD])
        cb2_sb = sb("cb2_sb", [P, KD])
        raw = [sb(f"fold_raw{i}", [P, KD, D]) for i in range(4)]
        folded = [sb(f"folded{i}", [P, KD, D]) for i in range(2)]
        ps_rank = ctx.enter_context(nc.psum_tensor("ps_rank", [NSEQ, 512], F32))
        ps_slot = ctx.enter_context(nc.psum_tensor("ps_slot", [P, 512], F32))
        ps_fold = [ctx.enter_context(nc.psum_tensor(f"ps_fold{i}", [P, D], F32)) for i in range(4)]

        small_in = sem("r_small_in")
        weights_in = [sem(f"r_weights_in{i}") for i in range(2)]
        made = sem("r_made")
        dve = sem("r_dve")
        ranks = sem("r_ranks")
        slots = sem("r_slots")
        fold_mm = sem("r_fold_mm")
        fold_ev = sem("r_fold_ev")
        stored = sem("r_stored")

        block = ctx.enter_context(nc.Block())

        @block.sync
        def _(sp):
            sp.dma_start(role_i[:], roles).then_inc(small_in, 16)
            sp.dma_start(codes_i[:], codes.broadcast_to([P, NSEQ])).then_inc(small_in, 16)
            sp.dma_start(cb2_sb[:], cb2).then_inc(small_in, 16)
            for i, w in enumerate((wqT, wkT, wvT, wp)):
                sp.dma_start(raw[i][:], w.rearrange("(k p) n -> p k n", p=P)).then_inc(weights_in[i // 2], 16)
            for f, dst in enumerate((fold_m, fold_v)):
                sp.wait_ge(fold_ev, KD * (f + 1))
                sp.dma_start(dst, folded[f][:].rearrange("p k n -> p (k n)")).then_inc(stored, 16)
            sp.wait_ge(stored, 32)

        @block.gpsimd
        def _(pool):
            pool.memset(ident[:], 0.0).then_inc(made, 1)
            pool.memset(before[:], 1.0).then_inc(made, 1)
            pool.memset(ones[:], 1.0).then_inc(made, 1)
            pool.iota(iota3[:], pattern=[[1, ROLES]], base=0, channel_multiplier=0,
                      allow_small_or_imprecise_dtypes=True).then_inc(made, 1)
            pool.iota(iota_slot[:], pattern=[[1, SLOTS]], base=0, channel_multiplier=0,
                      allow_small_or_imprecise_dtypes=True).then_inc(made, 1)
            pool.iota(iota_grp[:], pattern=[[GS, NG]], base=0, channel_multiplier=0,
                      allow_small_or_imprecise_dtypes=True).then_inc(made, 1)
            pool.iota(seq_off[:], pattern=[[0, 1]], base=-NSEQ, channel_multiplier=1,
                      allow_small_or_imprecise_dtypes=True).then_inc(made, 1)
            pool.iota(feat[:], pattern=[[P, KD]], base=0, channel_multiplier=1,
                      allow_small_or_imprecise_dtypes=True).then_inc(made, 1)
            pool.iota(slot_rows[:], pattern=[[P, NG]], base=NROWS, channel_multiplier=1,
                      allow_small_or_imprecise_dtypes=True).then_inc(made, 1)
            pool.wait_ge(made, 9)
            pool.affine_select(out=ident[:], in_=ident[:], compare_op=ALU.not_equal, fill=1.0,
                               base=0, pattern=[[-1, P]], channel_multiplier=1).then_inc(made, 1)
            pool.affine_select(out=before[:], in_=before[:], compare_op=ALU.is_gt, fill=0.0,
                               base=0, pattern=[[1, NSEQ]], channel_multiplier=-1).then_inc(made, 1)

        @block.vector
        def _(v):
            steps = [0]

            def step(ins):
                ins.then_inc(dve, 1)
                steps[0] += 1
                v.wait_ge(dve, steps[0])

            v.wait_ge(small_in, 48)
            v.wait_ge(made, 11)
            step(v.tensor_copy(role_f[:], role_i[:]))
            step(v.tensor_scalar(role_c[:], role_f[:], 0.0, float(ROLES - 1), ALU.max, ALU.min))
            step(v.tensor_scalar(onehot[:], iota3[:], role_c[:], None, ALU.is_equal))
            step(v.tensor_copy(codes_f[:], codes_i[:]))
            for m in range(KD):
                step(v.tensor_scalar(target_bias[:, m, :], codes_f[:], feat[:, m:m + 1],
                                     cb2_sb[:, m:m + 1], ALU.is_equal, ALU.add))
            v.wait_ge(ranks, 1)
            step(v.tensor_scalar(up_i[:], ps_rank[:, ROLES:2 * ROLES], float(GS - 1), None, ALU.add))
            step(v.tensor_scalar(up_r[:], up_i[:], -GS, None, ALU.bitwise_and))
            step(v.memset(base[:], 0.0))
            step(v.tensor_copy(base[:, 1:2], up_r[:, 0:1]))
            step(v.tensor_tensor(base[:, 2:3], base[:, 1:2], up_r[:, 1:2], ALU.add))
            step(v.tensor_tensor(place[:], base[:], ps_rank[:, 0:ROLES], ALU.add))
            step(v.tensor_tensor(placed[:], place[:], onehot[:], ALU.mult))
            step(v.reduce_sum(slot[:], placed[:], axis=AX))
            step(v.tensor_scalar(off_slot[:], iota_slot[:], -1.0, seq_off[:], ALU.mult, ALU.add))
            step(v.scalar_tensor_tensor(out=at_slot[:], in0=iota_slot[:], scalar=slot[:], in1=off_slot[:],
                                        op0=ALU.is_equal, op1=ALU.mult))
            step(v.tensor_copy(at_row[:], at_slot[:].rearrange("b (s a) -> b s a", a=1)
                               .broadcast_to([NSEQ, SLOTS, SROWS])))
            assert steps[0] == 19
            step(v.tensor_scalar(past1[:], iota_grp[:], base[0:1, 1:2], None, ALU.is_ge))
            step(v.tensor_scalar(past2[:], iota_grp[:], base[0:1, 2:3], None, ALU.is_ge))
            step(v.tensor_tensor(role_at[:], past1[:], past2[:], ALU.add))
            for layer in range(3):
                step(v.tensor_scalar(tab_row[:, layer * NG:(layer + 1) * NG], role_at[:],
                                     float(ROLES * layer), None, ALU.add))
            v.wait_ge(slots, 1)
            step(v.scalar_tensor_tensor(out=rows[:], in0=ps_slot[:, 0:NG], scalar=float(SROWS),
                                        in1=slot_rows[:], op0=ALU.mult, op1=ALU.add))
            step(v.tensor_copy(tab_dst[:, NG:2 * NG], rows[:]))
            for half in range(2):
                step(v.tensor_scalar(tab_src[:, half * NG:(half + 1) * NG], rows[:], float(NROWS - 1), None, ALU.min))
            step(v.tensor_copy(tab_dst[:, 0:NG], rows[:]))

        @block.tensor
        def _(pe):
            pe.wait_ge(made, 11)
            pe.wait_ge(dve, 3)
            pe.matmul(ps_rank[:, 0:ROLES], before[:], onehot[:], start=True, stop=True)
            pe.matmul(ps_rank[:, ROLES:2 * ROLES], ones[:], onehot[:], start=True, stop=True)\
                .then_inc(ranks, 1)
            for f in range(2):
                pe.wait_ge(weights_in[f], 32)
                for m in range(KD):
                    if f:
                        pe.wait_ge(fold_ev, KD * (f - 1) + m + 1)
                    for k in range(KD):
                        last = pe.matmul(ps_fold[m][:], raw[2 * f][:, k, m * P:(m + 1) * P],
                                         raw[2 * f + 1][:, k, :], start=(k == 0), stop=(k == KD - 1))
                    last.then_inc(fold_mm, 1)
                if f == 0:
                    pe.wait_ge(dve, 19)
                    for n in range(NG):
                        last = pe.matmul(ps_slot[:, n:n + 1], at_row[:, n * GS:(n + 1) * GS, :].rearrange("b s r -> b (s r)"),
                                         ones[:, 0:1], start=True, stop=True)
                    last.then_inc(slots, 1)

        @block.scalar
        def _(act):
            for f in range(2):
                for m in range(KD):
                    act.wait_ge(fold_mm, KD * f + m + 1)
                    act.activation(folded[f][:, m, :], ps_fold[m][:], ACT.Copy).then_inc(fold_ev, 1)


def ffn_layers(nc, tag, consts, layers, src, mid, dst, w_packed, rows_packed):
    tab_src, tab_dst, tab_row, _, ident = consts
    NJ = NG * len(layers)
    with ExitStack() as ctx:
        def sb(name, shape, dt=F32):
            return ctx.enter_context(nc.sbuf_tensor(f"{tag}_{name}", shape, dt))

        def pair(name, shape, dt=F32):
            return [sb(f"{name}{u}", shape, dt) for u in range(2)]

        def sem(name):
            return ctx.enter_context(nc.semaphore(f"{tag}_{name}"))

        src_row = pair("src_row", [P, 1], I32)
        dst_row = pair("dst_row", [P, 1], I32)
        row_ready = sem("row_ready")
        out_row_ready = sem("out_row_ready")
        x_tok = pair("x_tok", [P, GT, D])
        x_bias = pair("x_bias", [P, GT, D])
        xT_hi = sb("xT_hi", [P, KD, 512], F32R)
        xT_lo = sb("xT_lo", [P, KD, 512], F32R)
        w_raw = pair("w_raw", [P, WROW])
        wd_hi = pair("wd_hi", [P, KD, BN], F32R)
        wd_lo = pair("wd_lo", [P, KD, BN], F32R)
        wu_hi = pair("wu_hi", [P, KB, D], F32R)
        wu_lo = pair("wu_lo", [P, KB, D], F32R)
        bias_down = pair("bias_down", [P, KB])
        bias_up = pair("bias_up", [P, D])
        gain = pair("gain", [P, 2, D])
        g = pair("g", [P, 512])
        h_hi = pair("h_hi", [P, KB, 512], F32R)
        h_lo = pair("h_lo", [P, KB, 512], F32R)
        y = pair("y", [P, GT, D])
        z = pair("z", [P, D])
        stats = sb("stats", [P, GT, 6])
        mean_var = pair("mean_var", [P, GT, 2])
        var_eps = sb("var_eps", [P, GT])
        half = sb("half", [P, GT])
        neg_mean = sb("neg_mean", [P, GT])
        rstd = pair("rstd", [P, GT])
        shift = pair("shift", [P, GT])
        bank = [ctx.enter_context(nc.psum_tensor(f"{tag}_bank{i}", [P, 512], F32)) for i in range(8)]
        bank_T, bank_D, bank_U = bank[0:4], bank[4:6], bank[6:8]

        x_in = [sem(f"x_in{u}") for u in range(2)]
        w_in = [sem(f"w_in{u}") for u in range(2)]
        bup_in = [sem(f"bup_in{u}") for u in range(2)]
        gain_in = [sem(f"gain_in{u}") for u in range(2)]
        stored = [sem(f"stored{u}") for u in range(2)]
        tr_done = sem("tr_done")
        down_done = sem("down_done")
        up_done = sem("up_done")
        xhi_done = sem("xhi_done")
        xlo_done = sem("xlo_done")
        gelu_done = sem("gelu_done")
        hhi_done = sem("hhi_done")
        hlo_done = sem("hlo_done")
        wdhi_done = sem("wdhi_done")
        wuhi_done = sem("wuhi_done")
        wdlo_done = sem("wdlo_done")
        wulo_done = sem("wulo_done")
        xb_done = sem("xb_done")
        y_done = sem("y_done")
        bn_done = sem("bn_done")
        aggr_done = sem("aggr_done")
        met = sem("met")
        const_ready = sem("const_ready")
        small = sem("small")
        norm_done = sem("norm_done")
        mul_done = sem("mul_done")
        add_done = sem("add_done")

        def steps(eng, step):
            for j in range(4):
                step(j, j // 2, j % 2)
            with eng.Fori(2, NJ // 2 - 1) as h:
                step(2 * h, h, 0)
                step(2 * h + 1, h, 1)
            step(NJ - 2, NJ // 2 - 1, 0)
            step(NJ - 1, NJ // 2 - 1, 1)

        def is_int(j, *values):
            return isinstance(j, int) and j in values

        def settled(eng):
            eng.sem_inc(met, 1)

        block = ctx.enter_context(nc.Block())

        @block.sync
        def _(sp):
            def row_of(j):
                return sp.value_load(tab_row[0:1, bass.ds(j + NG * layers[0], 1)], min_val=0, max_val=3 * ROLES - 1)

            def load(j, h, u):
                row = row_of(j)
                sp.dma_start(w_raw[u][:], w_packed[bass.ds(row, 1)].rearrange("a p n -> (a p) n")).then_inc(w_in[u], 16)
                sp.dma_start(bias_up[u][:], rows_packed[bass.ds(row, 1), 0, :].broadcast_to([P, D])).then_inc(bup_in[u], 16)

            def load_gain(j, h, u):
                sp.dma_start(gain[u][:].rearrange("p a n -> p (a n)"),
                             rows_packed[bass.ds(row_of(j), 1), 1:3, :].rearrange("r a n -> r (a n)").broadcast_to([P, 2 * D]))\
                  .then_inc(gain_in[u], 16)

            load(0, 0, 0)
            load(1, 0, 1)

            def step(j, h, u):
                if not is_int(j, NJ - 2, NJ - 1):
                    sp.wait_ge(xb_done, j + 1)
                    sp.wait_ge(wdlo_done, j + 1)
                    sp.wait_ge(wdhi_done, 2 * j + 2)
                    sp.wait_ge(wulo_done, j + 1)
                    settled(sp)
                    load(j + 2, h + 1, u)
                if not is_int(j, 0, 1):
                    sp.wait_ge(add_done, GT * j - GT)
                    settled(sp)
                load_gain(j, h, u)
            steps(sp, step)

        @block.tensor
        def _(pe):
            def transposes(j, h, u):
                pe.wait_ge(x_in[u], 16 * (h + 1))
                for t in range(GT):
                    if not is_int(j, 0):
                        pe.wait_ge(xlo_done, GT * j - GT + t + 1)
                    for k in range(KD):
                        last = pe.transpose(bank_T[t][:, k * P:(k + 1) * P],
                                            x_tok[u][:, t, k * P:(k + 1) * P], ident[:])
                    last.then_inc(tr_done, 1)

            def down(j, h, u):
                pe.wait_ge(xlo_done, GT * j + GT)
                pe.wait_ge(wdlo_done, j + 1)
                for m in range(KB):
                    if not is_int(j, 0):
                        pe.wait_ge(gelu_done, KB * j - KB + m + 1)
                    ms = slice(m * P, (m + 1) * P)
                    product(pe, bank_D[m][:], [((wd_hi[u][:, k, ms], wd_lo[u][:, k, ms]),
                                                (xT_hi[:, k, :], xT_lo[:, k, :])) for k in range(KD)])\
                        .then_inc(down_done, 1)

            def up(j, h, u):
                pe.wait_ge(hlo_done, KB * j + KB)
                pe.wait_ge(wulo_done, j + 1)
                for t in range(GT):
                    if not (is_int(j, 0) and t < 2):
                        pe.wait_ge(y_done, GT * j + t - 1)
                    ts = slice(t * P, (t + 1) * P)
                    product(pe, bank_U[t % 2][:], [((h_hi[u][:, k, ts], h_lo[u][:, k, ts]),
                                                    (wu_hi[u][:, k, :], wu_lo[u][:, k, :])) for k in range(KB)])\
                        .then_inc(up_done, 1)

            transposes(0, 0, 0)

            def step(j, h, u):
                down(j, h, u)
                if not is_int(j, NJ - 1):
                    transposes(j + 1, h + u, 1 - u)
                if not is_int(j, 0):
                    up(j - 1, h - 1 + u, 1 - u)
            steps(pe, step)
            up(NJ - 1, NJ // 2 - 1, 1)

        @block.scalar
        def _(act):
            def split_down(j, h, u):
                act.wait_ge(w_in[u], 16 * (h + 1))
                act.activation(wd_hi[u][:].rearrange("p k n -> p (k n)"), w_raw[u][:, 0:KD * BN], ACT.Copy).then_inc(wdhi_done, 1)
                act.activation(bias_down[u][:], w_raw[u][:, KD * BN + KB * D:WROW], ACT.Copy).then_inc(wdhi_done, 1)

            def split_up(j, h, u):
                if not is_int(j, 0, 1):
                    act.wait_ge(up_done, GT * j - GT)
                act.activation(wu_hi[u][:].rearrange("p k n -> p (k n)"),
                               w_raw[u][:, KD * BN:KD * BN + KB * D], ACT.Copy).then_inc(wuhi_done, 1)

            def transposed_hi(j, h, u):
                for t in range(GT):
                    act.wait_ge(tr_done, GT * j + t + 1)
                    act.activation(xT_hi[:, :, t * P:(t + 1) * P],
                                   bank_T[t][:].rearrange("p (k t) -> p k t", k=KD), ACT.Copy).then_inc(xhi_done, 1)

            def gelu(j, h, u):
                act.wait_ge(wdhi_done, 2 * j + 2)
                for m in range(KB):
                    act.wait_ge(down_done, KB * j + m + 1)
                    if not is_int(j, 0):
                        act.wait_ge(hlo_done, KB * j - KB + m + 1)
                    act.activation(g[m][:], bank_D[m][:], ACT.Gelu, bias=bias_down[u][:, m:m + 1]).then_inc(gelu_done, 1)
                    act.wait_ge(gelu_done, KB * j + m + 1)
                    act.activation(h_hi[u][:, m, :], g[m][:], ACT.Copy).then_inc(hhi_done, 1)

            def norm(j, h, u):
                act.wait_ge(small, 4 * j + 4)
                for t in range(GT):
                    act.activation(y[u][:, t, :], y[u][:, t, :], ACT.Identity,
                                   scale=rstd[u][:, t:t + 1], bias=shift[u][:, t:t + 1]).then_inc(norm_done, 1)

            split_down(0, 0, 0)
            transposed_hi(0, 0, 0)

            def step(j, h, u):
                split_up(j, h, u)
                gelu(j, h, u)
                if not is_int(j, NJ - 1):
                    split_down(j + 1, h + u, 1 - u)
                    transposed_hi(j + 1, h + u, 1 - u)
                if not is_int(j, 0, 1):
                    norm(j - 2, h - 1, u)
            steps(act, step)
            norm(NJ - 2, NJ // 2 - 1, 0)
            norm(NJ - 1, NJ // 2 - 1, 1)

        @block.vector
        def _(v):
            def split_down(j, h, u):
                v.wait_ge(wdhi_done, 2 * j + 1)
                v.tensor_tensor(wd_lo[u][:].rearrange("p k n -> p (k n)"), w_raw[u][:, 0:KD * BN],
                                wd_hi[u][:].bitcast(F32).rearrange("p k n -> p (k n)"), ALU.subtract).then_inc(wdlo_done, 1)

            def split_up(j, h, u):
                v.wait_ge(wuhi_done, j + 1)
                v.tensor_tensor(wu_lo[u][:].rearrange("p k n -> p (k n)"), w_raw[u][:, KD * BN:KD * BN + KB * D],
                                   wu_hi[u][:].bitcast(F32).rearrange("p k n -> p (k n)"), ALU.subtract).then_inc(wulo_done, 1)

            def transposed_lo(j, h, u):
                for t in range(GT):
                    v.wait_ge(xhi_done, GT * j + t + 1)
                    v.tensor_tensor(xT_lo[:, :, t * P:(t + 1) * P], bank_T[t][:].rearrange("p (k t) -> p k t", k=KD),
                                    xT_hi[:, :, t * P:(t + 1) * P].bitcast(F32), ALU.subtract).then_inc(xlo_done, 1)

            def hidden_lo(j, h, u, m):
                v.wait_ge(hhi_done, KB * j + m + 1)
                v.tensor_tensor(h_lo[u][:, m, :], g[m][:], h_hi[u][:, m, :].bitcast(F32), ALU.subtract).then_inc(hlo_done, 1)

            def shift_gain(j, h, u, t):
                v.wait_ge(mul_done, GT * j + t + 1)
                v.tensor_tensor(y[u][:, t, :], z[t % 2][:], gain[u][:, 1, :], ALU.add).then_inc(add_done, 1)

            def residual(j, h, u, t):
                if t == 0:
                    v.wait_ge(xb_done, j + 1)
                    if not is_int(j, 0, 1):
                        v.wait_ge(stored[u], 16 * h)
                v.wait_ge(up_done, GT * j + t + 1)
                v.tensor_tensor(y[u][:, t, :], bank_U[t % 2][:], x_bias[u][:, t, :], ALU.add).then_inc(y_done, 1)

            def statistics(j, h, u, t):
                v.wait_ge(y_done, GT * j + t + 1)
                v.bn_stats(stats[:, t, :], y[u][:, t, :]).then_inc(bn_done, 1)

            def aggregate(j, h, u):
                v.wait_ge(bn_done, GT * j + GT)
                settled(v)
                for t in range(GT):
                    v.bn_aggr(mean_var[u][:, t, :], stats[:, t, :]).then_inc(aggr_done, 1)

            split_down(0, 0, 0)
            transposed_lo(0, 0, 0)

            def step(j, h, u):
                hidden_lo(j, h, u, 0)
                split_up(j, h, u)
                hidden_lo(j, h, u, 1)
                if not is_int(j, NJ - 1):
                    split_down(j + 1, h + u, 1 - u)
                    transposed_lo(j + 1, h + u, 1 - u)
                for t in range(GT):
                    if not is_int(j, 0):
                        residual(j - 1, h - 1 + u, 1 - u, t)
                    if not is_int(j, 0, 1):
                        shift_gain(j - 2, h - 1, u, t)
                    if not is_int(j, 0):
                        statistics(j - 1, h - 1 + u, 1 - u, t)
                if not is_int(j, 0):
                    aggregate(j - 1, h - 1 + u, 1 - u)
            steps(v, step)
            for t in range(GT):
                residual(NJ - 1, NJ // 2 - 1, 1, t)
                shift_gain(NJ - 2, NJ // 2 - 1, 0, t)
                statistics(NJ - 1, NJ // 2 - 1, 1, t)
            aggregate(NJ - 1, NJ // 2 - 1, 1)
            for t in range(GT):
                shift_gain(NJ - 1, NJ // 2 - 1, 1, t)

        @block.gpsimd
        def _(pool):
            def add_bias(j, h, u):
                pool.wait_ge(x_in[u], 16 * (h + 1))
                pool.wait_ge(bup_in[u], 16 * (h + 1))
                if not is_int(j, 0, 1):
                    pool.wait_ge(y_done, GT * j - GT)
                pool.tensor_tensor(x_bias[u][:], x_tok[u][:],
                                   bias_up[u][:].rearrange("p (a n) -> p a n", a=1).broadcast_to([P, GT, D]),
                                   ALU.add).then_inc(xb_done, 1)

            def rstd_shift(j, h, u):
                pool.wait_ge(aggr_done, GT * j + GT)
                settled(pool)
                pool.tensor_scalar(var_eps[:], mean_var[u][:, :, 1], LN_EPS, None, ALU.add).then_inc(small, 1)
                pool.tensor_scalar(neg_mean[:], mean_var[u][:, :, 0], -1.0, None, ALU.mult).then_inc(small, 1)
                pool.wait_ge(const_ready, 1)
                pool.wait_ge(small, 4 * j + 2)
                pool.tensor_tensor(rstd[u][:], var_eps[:], half[:], ALU.pow).then_inc(small, 1)
                pool.wait_ge(small, 4 * j + 3)
                pool.tensor_tensor(shift[u][:], neg_mean[:], rstd[u][:], ALU.mult).then_inc(small, 1)

            def multiply_gain(j, h, u):
                pool.wait_ge(gain_in[u], 16 * (h + 1))
                for t in range(GT):
                    pool.wait_ge(norm_done, GT * j + t + 1)
                    if not (is_int(j, 0) and t < 2):
                        pool.wait_ge(add_done, GT * j + t - 1)
                    pool.tensor_tensor(z[t % 2][:], y[u][:, t, :], gain[u][:, 0, :], ALU.mult).then_inc(mul_done, 1)

            def either(j, first, second):
                if len(layers) == 1:
                    first()
                elif isinstance(j, int):
                    (first if j < NG else second)()
                else:
                    with pool.If(j < NG):
                        first()
                    with pool.Else():
                        second()

            def gather(j, h, u):
                pool.tensor_copy(src_row[u][:], tab_src[:, bass.ds(j, 1)]).then_inc(row_ready, 1)
                pool.wait_ge(row_ready, j + 1)
                settled(pool)
                to = x_tok[u][:].rearrange("p t n -> p (t n)")

                def sequences():
                    pool.indirect_dma_start(out=to, out_offset=None, in_=src,
                                            in_offset=bass.IndirectOffsetOnAxis(ap=src_row[u][:], axis=0)).then_inc(x_in[u], 16)

                def first_layers():
                    pool.dma_start(to, mid[bass.ds(j * P, P), :]).then_inc(x_in[u], 16)
                either(j, sequences, first_layers)

            def scatter(j, h, u):
                pool.wait_ge(add_done, GT * j + GT)
                pool.tensor_copy(dst_row[u][:], tab_dst[:, bass.ds(j + NG * (2 - len(layers)), 1)]).then_inc(out_row_ready, 1)
                pool.wait_ge(out_row_ready, j + 1)
                settled(pool)
                of = y[u][:].rearrange("p t n -> p (t n)")

                def first_layers():
                    pool.dma_start(mid[bass.ds((j + NG) * P, P), :], of).then_inc(stored[u], 16)

                def sequences():
                    pool.indirect_dma_start(out=dst, out_offset=bass.IndirectOffsetOnAxis(ap=dst_row[u][:], axis=0),
                                            in_=of, in_offset=None).then_inc(stored[u], 16)
                either(j, first_layers if len(layers) > 1 else sequences, sequences)

            pool.memset(half[:], -0.5).then_inc(const_ready, 1)
            gather(0, 0, 0)
            gather(1, 0, 1)

            def step(j, h, u):
                add_bias(j, h, u)
                if not is_int(j, NJ - 2, NJ - 1):
                    pool.wait_ge(tr_done, GT * j + GT)
                    pool.wait_ge(xb_done, j + 1)
                    gather(j + 2, h + 1, u)
                if not is_int(j, 0, 1):
                    multiply_gain(j - 2, h - 1, u)
                    scatter(j - 2, h - 1, u)
                if not is_int(j, 0):
                    rstd_shift(j - 1, h - 1 + u, 1 - u)
            steps(pool, step)
            multiply_gain(NJ - 2, NJ // 2 - 1, 0)
            scatter(NJ - 2, NJ // 2 - 1, 0)
            rstd_shift(NJ - 1, NJ // 2 - 1, 1)
            multiply_gain(NJ - 1, NJ // 2 - 1, 1)
            scatter(NJ - 1, NJ // 2 - 1, 1)
            for u in range(2):
                pool.wait_ge(stored[u], 16 * (NJ // 2))


def core_layer(nc, consts, units_a, units_b, units_c, fold_m, fold_v, bias_cols, src, dst):
    _, _, _, target_bias, ident = consts
    NA, NBU, NC = 2 * CH + 1, 2 * CH + 1, CH
    TILES = KD * NH
    HTILES = 2 * CH * TILES
    with ExitStack() as ctx:
        place = [nc.sbuf_base]

        def sb(name, shape, dt=F32, at=None):
            size = 1
            for x in shape[1:]:
                size *= x
            if at is None:
                at = (place[0] + 31) // 32 * 32
                place[0] = at + 4 * size
                where[name] = at
            return nc.alloc_sbuf_tensor_at(name, shape, dt, offset=at)

        where = {}

        def sem(name):
            return ctx.enter_context(nc.semaphore(name))

        x_tok = sb("x_tok", [P, TT, D])
        base = x_tok[:].rearrange("p t n -> p (t n)")
        cms = base.rearrange("p (k n) -> p k n", k=KD)
        acc = sb("acc", [P, KD, SBT])
        xc_hi = sb("xc_hi", [P, KD, SBT], F32R)
        xc_lo = sb("xc_lo", [P, KD, SBT], F32R)
        o_hi = sb("o_hi", [P, KD, SBT], F32R)
        o_lo = sb("o_lo", [P, KD, SBT], F32R)
        h_hi = sb("h_hi", [P, KD, SBT], F32R)
        h_lo = sb("h_lo", [P, KD, SBT], F32R)
        a_hi = h_hi[:].rearrange("p k n -> p (k n)")[:, 0:KD * 512].rearrange("p (k n) -> p k n", k=KD)
        a_lo = h_lo[:].rearrange("p k n -> p (k n)")[:, 0:KD * 512].rearrange("p (k n) -> p k n", k=KD)
        yT = sb("yT", [P, KD, 512], at=where["h_hi"] + 4 * KD * 512)
        stage = sb("stage", [P, 2, D])
        w_raw = [sb(f"w_raw{i}", [P, KD * D]) for i in range(2)]
        w_hi = {s: sb(f"w_hi{s}", [P, KD, D], F32R) for s in "ABC"}
        w_lo = {s: sb(f"w_lo{s}", [P, KD, D], F32R) for s in "ABC"}
        g = [sb(f"g{i}", [P, 512]) for i in range(2)]
        probs = sb("probs", [P, HT, P])
        probsT = sb("probsT", [P, HT, P])
        row_max = sb("row_max", [P, HT])
        row_sum = sb("row_sum", [P, HT])
        row_inv = sb("row_inv", [P, HT])
        expd = sb("expd", [P, HT, LEN])
        bias = sb("bias_cols", [P, 2 * HID // P + 2 * KD])
        cb1, mb1 = bias[:, 0:HID // P], bias[:, HID // P:2 * HID // P]
        bp, mb2 = bias[:, 2 * HID // P:2 * HID // P + KD], bias[:, 2 * HID // P + KD:]
        bank = [ctx.enter_context(nc.psum_tensor(f"bank{i}", [P, 512], F32)) for i in range(8)]

        raw_in = [sem(f"raw_in{i}") for i in range(2)]
        x_in = sem("x_in")
        bias_in = sem("bias_in")
        stored = [sem(f"stored{i}") for i in range(2)]
        hi_done = {s: sem(f"hi_done{s}") for s in "ABC"}
        lo_done = {s: sem(f"lo_done{s}") for s in "ABC"}
        tr_done = sem("tr_done")
        xraw_done = sem("xraw_done")
        xhi_done = sem("xhi_done")
        xlo_done = sem("xlo_done")
        y_mm = sem("y_mm")
        y_done = sem("y_done")
        s_mm = sem("s_mm")
        max_done = sem("max_done")
        sub_done = sem("sub_done")
        exp_done = sem("exp_done")
        sum_done = sem("sum_done")
        inv_done = sem("inv_done")
        zeroed = sem("zeroed")
        probs_done = sem("probs_done")
        pt_mm = sem("pt_mm")
        pt_done = sem("pt_done")
        av_mm = sem("av_mm")
        ahi_done = sem("ahi_done")
        alo_done = sem("alo_done")
        o_mm = sem("o_mm")
        ohi_done = sem("ohi_done")
        olo_done = sem("olo_done")
        init_done = sem("init_done")
        hid_mm = sem("hid_mm")
        gelu_done = sem("gelu_done")
        hhi_done = sem("hhi_done")
        hlo_done = sem("hlo_done")
        out_mm = sem("out_mm")
        acc_done = sem("acc_done")
        chi_done = sem("chi_done")
        clo_done = sem("clo_done")
        sum_ready = sem("sum_ready")
        fin_mm = sem("fin_mm")
        fin_done = sem("fin_done")
        met = sem("met")

        def settled(eng):
            eng.sem_inc(met, 1)

        def cols(n):
            return slice(n * 512, (n + 1) * 512)

        block = ctx.enter_context(nc.Block())

        @block.sync
        def _(sp):
            def load_a(s, k, unit):
                if not (isinstance(s, int) and s == 0 and k == 0):
                    sp.wait_ge(lo_done["A"], NA * s + k)
                sp.dma_start(w_raw[0][:], unit).then_inc(raw_in[0], 16)

            def load_bc(s, before_b, before_c, unit):
                sp.wait_ge(lo_done["B"], NBU * s + before_b)
                settled(sp)
                sp.wait_ge(lo_done["C"], NC * s + before_c)
                sp.dma_start(w_raw[1][:], unit).then_inc(raw_in[1], 16)

            def load_x(s):
                sp.dma_start(x_tok[:], src[bass.ds(s * SBT, SBT), :].rearrange("(t p) n -> p t n", p=P)).then_inc(x_in, 16)

            sp.dma_start(bias[:], bias_cols).then_inc(bias_in, 16)
            load_x(0)
            load_a(0, 0, fold_m)
            sp.dma_start(w_raw[1][:], fold_v).then_inc(raw_in[1], 16)
            sp.wait_ge(lo_done["B"], 1)
            sp.dma_start(w_raw[1][:], units_c[0]).then_inc(raw_in[1], 16)

            def super_block(s, more):
                load_a(s, 1, units_a[0])
                load_bc(s, 1, 1, units_b[0])
                for c in range(CH):
                    load_a(s, 2 + c, units_a[1 + c])
                    load_bc(s, 2 + c, 1, units_b[1 + c])
                for c in range(CH):
                    load_a(s, 2 + CH + c, units_a[1 + CH + c] if c < CH - 1 else fold_m)
                    load_bc(s, 2 + CH + c, 1 + c, units_c[(c + 1) % CH])
                    load_bc(s, 2 + CH + c, 2 + c, units_b[1 + CH + c] if c < CH - 1 else fold_v)
                    if more and c == 0:
                        sp.wait_ge(sum_ready, TILES * s + TILES)
                        load_x(s + 1)
                for t in range(TT):
                    sp.wait_ge(fin_done, TT * s + t + 1)
                    sp.dma_start(dst[bass.ds(s * SBT + t * P, P), :], stage[:, t % 2, :]).then_inc(stored[t % 2], 16)
                for i in range(2):
                    sp.wait_ge(stored[i], 8 * TT * s + 8 * TT)
                    settled(sp)

            with sp.Fori(0, SB - 1) as s:
                super_block(s, True)
            super_block(SB - 1, False)

        @block.tensor
        def _(pe):
            def unit_terms(slot, m, hi, lo, n):
                ms = slice(m * P, (m + 1) * P)
                return [((w_hi[slot][:, k, ms], w_lo[slot][:, k, ms]), (hi[:, k, cols(n)], lo[:, k, cols(n)]))
                        for k in range(KD)]

            def super_block(s):
                pe.wait_ge(x_in, 16 * s + 16)
                for t in range(TT):
                    for k in range(KD):
                        last = pe.transpose(bank[t][:, k * P:(k + 1) * P], x_tok[:, t, k * P:(k + 1) * P], ident[:])
                    last.then_inc(tr_done, 1)

                def query(n):
                    pe.wait_ge(xlo_done, TT * s + HT * (n + 1))
                    for m in range(KD):
                        product(pe, bank[m][:], unit_terms("A", m, xc_hi, xc_lo, n)).then_inc(y_mm, 1)

                def scores(n):
                    pe.wait_ge(y_done, TILES * s + KD * (n + 1))
                    if n == 0:
                        pe.wait_ge(xlo_done, TT * s + HT + 1)
                    for i in range(HT):
                        t = HT * n + i
                        for k in range(KD):
                            last = pe.matmul(bank[4 + n][:, i * P:(i + 1) * P], yT[:, k, i * P:(i + 1) * P],
                                             acc[:, k, t * P:(t + 1) * P], start=(k == 0), stop=(k == KD - 1))
                    last.then_inc(s_mm, 1)

                def turn_probs(n):
                    pe.wait_ge(probs_done, 2 * NH * s + 2 * (n + 1))
                    for i in range(HT):
                        last = pe.transpose(bank[6 + n][:, i * P:(i + 1) * P], probs[:, i, :], ident[:])
                    last.then_inc(pt_mm, 1)

                def attend(n):
                    pe.wait_ge(pt_done, NH * s + n + 1)
                    for i in range(HT):
                        for k in range(KD):
                            last = pe.matmul(bank[i][:, k * P:(k + 1) * P], x_tok[:, HT * n + i, k * P:(k + 1) * P],
                                             probsT[:, i, :], start=True, stop=True)
                        last.then_inc(av_mm, 1)

                def output(n):
                    pe.wait_ge(alo_done, TT * s + HT * (n + 1))
                    for m in range(KD):
                        if n or m >= 2:
                            pe.wait_ge(olo_done, TILES * s + KD * n + m - 1)
                        ms = slice(m * P, (m + 1) * P)
                        product(pe, bank[4 + 2 * (m % 2)][:],
                                [((w_hi["B"][:, k, ms], w_lo["B"][:, k, ms]), (a_hi[:, k, :], a_lo[:, k, :]))
                                 for k in range(KD)]).then_inc(o_mm, 1)

                pe.wait_ge(lo_done["A"], NA * s + 1)
                query(0)
                scores(0)
                query(1)
                turn_probs(0)
                scores(1)
                attend(0)
                pe.wait_ge(lo_done["B"], NBU * s + 1)
                output(0)
                turn_probs(1)
                attend(1)
                output(1)

                def hidden(c, q, units):
                    n, j = q % NH, q // NH
                    if q >= 4:
                        pe.wait_ge(gelu_done, HTILES * s + TILES * c + q - 3)
                    product(pe, bank[q % 4][:], units(j, n)).then_inc(hid_mm, 1)

                def out_tiles(c, slot_b):
                    pe.wait_ge(lo_done["B"], slot_b)
                    for n in range(NH):
                        pe.wait_ge(hlo_done, HTILES * s + TILES * c + TILES - NH + 1 + n)
                        for m in range(KD):
                            r = KD * n + m
                            if r >= 4:
                                pe.wait_ge(acc_done, HTILES * s + TILES * c + r - 3)
                            product(pe, bank[4 + r % 4][:], unit_terms("B", m, h_hi, h_lo, n)).then_inc(out_mm, 1)

                with pe.Fori(0, CH) as c:
                    pe.wait_ge(lo_done["A"], NA * s + c + 2)
                    for q in range(TILES):
                        if q < NH:
                            pe.wait_ge(olo_done, TILES * s + KD * (q + 1))
                        hidden(c, q, lambda j, n: unit_terms("A", j, o_hi, o_lo, n))
                    out_tiles(c, NBU * s + c + 2)
                with pe.Fori(0, CH) as c:
                    pe.wait_ge(lo_done["A"], NA * s + c + 2 + CH)
                    pe.wait_ge(lo_done["C"], NC * s + c + 1)
                    for q in range(TILES):
                        if q < NH:
                            n = q
                            first = unit_terms("A", 0, o_hi, o_lo, n)
                            second = unit_terms("C", 0, xc_hi, xc_lo, n)
                            for i, ((lh, ll), (rh, rl)) in enumerate(first + second):
                                if i == KD:
                                    pe.wait_ge(clo_done, TILES * s + KD * (n + 1))
                                pe.matmul(bank[q][:], lh, rh, start=(i == 0), stop=False)
                                pe.matmul(bank[q][:], lh, rl, start=False, stop=False)
                                last = pe.matmul(bank[q][:], ll, rh, start=False, stop=(i == 2 * KD - 1))
                            last.then_inc(hid_mm, 1)
                        else:
                            hidden(c + CH, q, lambda j, n: unit_terms("A", j, o_hi, o_lo, n)
                                   + unit_terms("C", j, xc_hi, xc_lo, n))
                    out_tiles(c + CH, NBU * s + c + 2 + CH)

                for t in range(TT):
                    if t % HT == 0:
                        pe.wait_ge(acc_done, HTILES * (s + 1) - TILES + KD * (t // HT + 1))
                    for m in range(KD):
                        last = pe.transpose(bank[t][:, m * P:(m + 1) * P], acc[:, m, t * P:(t + 1) * P], ident[:])
                    last.then_inc(fin_mm, 1)
                pe.wait_ge(fin_done, TT * s + TT)

            with pe.Fori(0, SB) as s:
                super_block(s)

        @block.scalar
        def _(act):
            def split(slot, n_raw):
                i = 0 if slot == "A" else 1
                act.wait_ge(raw_in[i], 16 * n_raw)
                act.activation(w_hi[slot][:].rearrange("p k n -> p (k n)"), w_raw[i][:], ACT.Copy).then_inc(hi_done[slot], 1)

            def super_block(s):
                nb = (NBU + NC) * s
                for t in range(TT):
                    act.wait_ge(tr_done, TT * s + t + 1)
                    tile = bank[t][:].rearrange("p (k t) -> p k t", k=KD)
                    act.activation(acc[:, :, t * P:(t + 1) * P], tile, ACT.Copy).then_inc(xraw_done, 1)
                    act.activation(xc_hi[:, :, t * P:(t + 1) * P], tile, ACT.Copy).then_inc(xhi_done, 1)

                def query(n):
                    for m in range(KD):
                        act.wait_ge(y_mm, TILES * s + KD * n + m + 1)
                        act.activation(yT[:, m, :], bank[m][:], ACT.Copy).then_inc(y_done, 1)

                def softmax(n):
                    act.wait_ge(sub_done, 2 * NH * s + 2 * (n + 1))
                    act.activation(expd[:], expd[:], ACT.Exp, scale=SCALE).then_inc(exp_done, 1)

                def turned(n):
                    act.wait_ge(pt_mm, NH * s + n + 1)
                    act.activation(probsT[:].rearrange("p i t -> p (i t)"), bank[6 + n][:], ACT.Copy).then_inc(pt_done, 1)

                def attended(n):
                    for i in range(HT):
                        act.wait_ge(av_mm, TT * s + HT * n + i + 1)
                        act.activation(a_hi[:, :, i * P:(i + 1) * P], bank[i][:].rearrange("p (k t) -> p k t", k=KD),
                                       ACT.Copy).then_inc(ahi_done, 1)

                def output(n):
                    for m in range(KD):
                        act.wait_ge(o_mm, TILES * s + KD * n + m + 1)
                        act.activation(o_hi[:, m, cols(n)], bank[4 + 2 * (m % 2)][:], ACT.Identity,
                                       bias=bp[:, m:m + 1]).then_inc(ohi_done, 1)

                query(0)
                query(1)
                softmax(0)
                turned(0)
                split("A", NA * s + 2)
                attended(0)
                softmax(1)
                output(0)
                turned(1)
                attended(1)
                output(1)
                split("B", nb + 3)

                def chunk(c, bias_at):
                    for q in range(TILES):
                        n, j = q % NH, q // NH
                        at = HTILES * s + TILES * c + q + 1
                        act.wait_ge(hid_mm, at)
                        if q >= 2:
                            act.wait_ge(hlo_done, at - 2)
                        settled(act)
                        act.activation(g[q % 2][:], bank[q % 4][:], ACT.Gelu,
                                       bias=bias_at(j)).then_inc(gelu_done, 1)
                        act.wait_ge(gelu_done, at)
                        act.activation(h_hi[:, j, cols(n)], g[q % 2][:], ACT.Copy).then_inc(hhi_done, 1)

                with act.Fori(0, CH) as c:
                    chunk(c, lambda j: cb1[:, bass.ds(c * KD + j, 1)])
                    split("A", NA * s + c + 3)
                    act.wait_ge(out_mm, HTILES * s + TILES * c + TILES)
                    split("B", nb + c + 4)
                for r in range(TILES):
                    n, m = r // KD, r % KD
                    act.wait_ge(acc_done, HTILES * s + TILES * (CH - 1) + r + 1)
                    act.activation(xc_hi[:, m, cols(n)], cms[:, m, cols(n)], ACT.Copy).then_inc(chi_done, 1)
                with act.Fori(0, CH) as c:
                    chunk(c + CH, lambda j: mb1[:, bass.ds(c * KD + j, 1)])
                    split("A", NA * s + c + 3 + CH)
                    split("C", nb + 2 * c + 4 + CH)
                    act.wait_ge(out_mm, HTILES * s + TILES * (c + CH) + TILES)
                    split("B", nb + 2 * c + 5 + CH)

            act.wait_ge(bias_in, 16)
            split("A", 1)
            split("B", 1)
            split("C", 2)
            with act.Fori(0, SB) as s:
                super_block(s)

        @block.vector
        def _(v):
            def split(slot, n):
                i = 0 if slot == "A" else 1
                v.wait_ge(hi_done[slot], n)
                v.tensor_tensor(w_lo[slot][:].rearrange("p k n -> p (k n)"), w_raw[i][:],
                                w_hi[slot][:].bitcast(F32).rearrange("p k n -> p (k n)"), ALU.subtract).then_inc(lo_done[slot], 1)

            def super_block(s):
                for t in range(TT):
                    v.wait_ge(xhi_done, TT * s + t + 1)
                    v.tensor_tensor(xc_lo[:, :, t * P:(t + 1) * P], bank[t][:].rearrange("p (k t) -> p k t", k=KD),
                                    xc_hi[:, :, t * P:(t + 1) * P].bitcast(F32), ALU.subtract).then_inc(xlo_done, 1)

                def softmax(n):
                    v.wait_ge(s_mm, NH * s + n + 1)
                    at = NH * s + n
                    tile = bank[4 + n][:].rearrange("p (i t) -> p i t", i=HT)
                    for q in range(2):
                        ps = slice(q * LEN, (q + 1) * LEN)
                        v.reduce_max(row_max[ps, :], tile[ps, :, ps], axis=AX).then_inc(max_done, 1)
                    v.wait_ge(max_done, 2 * at + 2)
                    for q in range(2):
                        ps = slice(q * LEN, (q + 1) * LEN)
                        v.tensor_tensor(expd[ps, :, :], tile[ps, :, ps],
                                        row_max[ps, :].rearrange("p (i a) -> p i a", a=1).broadcast_to([LEN, HT, LEN]),
                                        ALU.subtract).then_inc(sub_done, 1)
                    v.wait_ge(exp_done, at + 1)
                    v.reduce_sum(row_sum[:], expd[:], axis=AX).then_inc(sum_done, 1)
                    v.wait_ge(sum_done, at + 1)
                    v.reciprocal(row_inv[:], row_sum[:]).then_inc(inv_done, 1)
                    v.wait_ge(inv_done, at + 1)
                    for q in range(2):
                        ps = slice(q * LEN, (q + 1) * LEN)
                        v.tensor_tensor(probs[ps, :, ps], expd[ps, :, :],
                                        row_inv[ps, :].rearrange("p (i a) -> p i a", a=1).broadcast_to([LEN, HT, LEN]),
                                        ALU.mult).then_inc(probs_done, 1)

                def attended(n):
                    for i in range(HT):
                        v.wait_ge(ahi_done, TT * s + HT * n + i + 1)
                        cs = slice(i * P, (i + 1) * P)
                        v.tensor_tensor(a_lo[:, :, cs], bank[i][:].rearrange("p (k t) -> p k t", k=KD),
                                        a_hi[:, :, cs].bitcast(F32), ALU.subtract).then_inc(alo_done, 1)

                def output(n):
                    for m in range(KD):
                        v.wait_ge(ohi_done, TILES * s + KD * n + m + 1)
                        v.scalar_tensor_tensor(out=o_lo[:, m, cols(n)], in0=bank[4 + 2 * (m % 2)][:],
                                               scalar=bp[:, m:m + 1], in1=o_hi[:, m, cols(n)].bitcast(F32),
                                               op0=ALU.add, op1=ALU.subtract).then_inc(olo_done, 1)

                softmax(0)
                split("A", NA * s + 2)
                attended(0)
                softmax(1)
                output(0)
                attended(1)
                output(1)
                split("B", NBU * s + 2)

                def hidden_lo(c):
                    for q in range(TILES):
                        n, j = q % NH, q // NH
                        v.wait_ge(hhi_done, HTILES * s + TILES * c + q + 1)
                        v.tensor_tensor(h_lo[:, j, cols(n)], g[q % 2][:], h_hi[:, j, cols(n)].bitcast(F32),
                                        ALU.subtract).then_inc(hlo_done, 1)

                def accumulate(c, into):
                    for r in range(TILES):
                        n, m = r // KD, r % KD
                        v.wait_ge(out_mm, HTILES * s + TILES * c + r + 1)
                        v.tensor_tensor(into[:, m, cols(n)], bank[4 + r % 4][:], into[:, m, cols(n)],
                                        ALU.add).then_inc(acc_done, 1)

                with v.Fori(0, CH) as c:
                    hidden_lo(c)
                    split("A", NA * s + c + 3)
                    v.wait_ge(init_done, KD * s + KD)
                    accumulate(c, cms)
                    split("B", NBU * s + c + 3)
                for r in range(TILES):
                    n, m = r // KD, r % KD
                    v.wait_ge(chi_done, TILES * s + r + 1)
                    v.tensor_tensor(xc_lo[:, m, cols(n)], cms[:, m, cols(n)], xc_hi[:, m, cols(n)].bitcast(F32),
                                    ALU.subtract).then_inc(clo_done, 1)
                for r in range(TILES):
                    n, m = r // KD, r % KD
                    v.scalar_tensor_tensor(out=acc[:, m, cols(n)], in0=cms[:, m, cols(n)], scalar=mb2[:, m:m + 1],
                                           in1=acc[:, m, cols(n)], op0=ALU.add, op1=ALU.add).then_inc(sum_ready, 1)
                v.wait_ge(sum_ready, TILES * s + TILES)
                settled(v)
                with v.Fori(0, CH) as c:
                    hidden_lo(c + CH)
                    split("A", NA * s + c + 3 + CH)
                    split("C", NC * s + c + 2)
                    accumulate(c + CH, acc)
                    split("B", NBU * s + c + 3 + CH)
                for t in range(TT):
                    v.wait_ge(fin_mm, TT * s + t + 1)
                    if t >= 2:
                        v.wait_ge(stored[t % 2], 16 * (TT // 2) * s + 16 * (t // 2))
                    v.tensor_scalar(stage[:, t % 2, :], bank[t][:], 0.0, 1.0, ALU.max, ALU.min).then_inc(fin_done, 1)

            v.wait_ge(bias_in, 16)
            v.wait_ge(zeroed, 1)
            split("A", 1)
            split("B", 1)
            split("C", 1)
            with v.Fori(0, SB) as s:
                super_block(s)

        @block.gpsimd
        def _(pool):
            pool.memset(probs[:], 0.0).then_inc(zeroed, 1)
            with pool.Fori(0, SB) as s:
                pool.wait_ge(av_mm, TT * s + TT)
                for m in range(KD):
                    pool.tensor_copy(cms[:, m, :].rearrange("p (b l) -> p b l", l=LEN),
                                     target_bias[:, m, bass.ds(s * SEQ_SB, SEQ_SB)]
                                     .rearrange("p (b a) -> p b a", a=1).broadcast_to([P, SEQ_SB, LEN]))\
                        .then_inc(init_done, 1)


def packed_linear(a):
    import numpy as np
    *lead, rows, n = a.shape
    a = a.reshape(*lead, rows // P, P, n)
    return np.swapaxes(a, -3, -2).reshape(*lead, P, rows // P * n)


def column_tiles(a):
    import numpy as np
    return np.ascontiguousarray(a.reshape(-1, P).T)


def build(nc, x, roles, codes, cb2, wqT, wkT, wvT, wp, w_packed, rows_packed,
          units_a, units_b, units_c, bias_cols, out):
    def scratch(name, shape):
        return nc.dram_tensor(name, shape, F32, kind="Internal").ap()

    fold_m = scratch("fold_m", (P, KD * D))
    fold_v = scratch("fold_v", (P, KD * D))
    x1 = scratch("x1", (NROWS + NG * P, GT * D))
    x2 = scratch("x2", (NROWS, GT * D))
    mid = scratch("mid", (3 * NG * P, GT * D))
    with ExitStack() as ctx:
        def sb(name, shape, dt=F32):
            return ctx.enter_context(nc.sbuf_tensor(name, shape, dt))

        consts = (sb("tab_src", [P, 2 * NG], I32), sb("tab_dst", [P, 2 * NG], I32), sb("tab_row", [1, 3 * NG], I32),
                  sb("target_bias", [P, KD, NSEQ]), sb("ident", [P, P]))
        route_and_fold(nc, consts, roles, codes, cb2, wqT, wkT, wvT, wp, fold_m, fold_v)
        ffn_layers(nc, "first", consts, (0,), x, None, x1, w_packed, rows_packed)
        core_layer(nc, consts, units_a, units_b, units_c, fold_m, fold_v, bias_cols,
                   x1.rearrange("a (t n) -> (a t) n", n=D), x2.rearrange("a (t n) -> (a t) n", n=D))
        ffn_layers(nc, "last", consts, (1, 2), x2, mid, out, w_packed, rows_packed)


def kernel(x, itok_B_1_2, itok_B_17_1546, _lenS,
           L0_cond_W_down, L0_cond_b_down, L0_cond_W_up, L0_cond_b_up, L0_cond_gamma, L0_cond_beta,
           L1_cond_Wq, L1_cond_Wk, L1_cond_Wv, L1_cond_Wp, L1_cond_bp, L1_cond_cW1, L1_cond_cb1,
           L1_cond_cW2, L1_cond_cb2, L1_cond_mW1, L1_cond_mb1, L1_cond_mW2, L1_cond_mb2,
           L2_cond_W_down, L2_cond_b_down, L2_cond_W_up, L2_cond_b_up, L2_cond_gamma, L2_cond_beta,
           L3_cond_W_down, L3_cond_b_down, L3_cond_W_up, L3_cond_b_up, L3_cond_ln_w, L3_cond_ln_b):
    import numpy as np
    import concourse.bacc as bacc
    from concourse.bass_utils import run_bass_kernel_spmd

    def both(*arrays):
        return np.concatenate([np.asarray(a) for a in arrays])

    w_down = both(L0_cond_W_down, L2_cond_W_down, L3_cond_W_down)
    w_up = both(L0_cond_W_up, L2_cond_W_up, L3_cond_W_up)
    b_down = both(L0_cond_b_down, L2_cond_b_down, L3_cond_b_down)
    b_up = both(L0_cond_b_up, L2_cond_b_up, L3_cond_b_up)
    gamma = both(L0_cond_gamma, L2_cond_gamma, L3_cond_ln_w)
    beta = both(L0_cond_beta, L2_cond_beta, L3_cond_ln_b)
    w_packed = np.concatenate([packed_linear(w_down), packed_linear(w_up),
                               np.stack([column_tiles(b) for b in b_down])], axis=-1)
    cw1, cw2, mw1, mw2 = (np.asarray(a) for a in (L1_cond_cW1, L1_cond_cW2, L1_cond_mW1, L1_cond_mW2))
    chunks = [slice(c * D, (c + 1) * D) for c in range(CH)]
    host = {
        "x": np.asarray(x).reshape(NROWS, GT * D),
        "roles": np.asarray(itok_B_1_2).reshape(NSEQ, 1),
        "codes": np.asarray(itok_B_17_1546).reshape(1, NSEQ),
        "cb2": column_tiles(np.asarray(L1_cond_cb2)),
        "wqT": np.asarray(L1_cond_Wq).T, "wkT": np.asarray(L1_cond_Wk).T,
        "wvT": np.asarray(L1_cond_Wv).T, "wp": np.asarray(L1_cond_Wp),
        "w_packed": w_packed,
        "rows_packed": np.stack([b_up, gamma, beta], axis=1),
        "units_a": packed_linear(np.stack([cw1[:, c] for c in chunks] + [mw1[:D, c] for c in chunks])),
        "units_b": packed_linear(np.stack([cw2[c] for c in chunks] + [mw2[c] for c in chunks])),
        "units_c": packed_linear(np.stack([mw1[D:, c] for c in chunks])),
        "bias_cols": np.concatenate([column_tiles(np.asarray(a)) for a in
                                     (L1_cond_cb1, L1_cond_mb1, L1_cond_bp, L1_cond_mb2)], axis=1),
    }
    nc = bacc.Bacc("TRN2", target_bir_lowering=False, num_devices=1)
    arrays, args = {}, {}
    for name, a in host.items():
        arrays[f"in_{name}"] = np.ascontiguousarray(a)
        args[name] = nc.dram_tensor(f"in_{name}", a.shape, mybir.dt.from_np(a.dtype), kind="ExternalInput").ap()
    out = nc.dram_tensor("out_rows", (NROWS + NG * P, GT * D), F32, kind="ExternalOutput").ap()
    build(nc, **args, out=out)
    r = run_bass_kernel_spmd(nc, [arrays], core_ids=[0])
    return r.results[0]["out_rows"][:NROWS].reshape(NSEQ, LEN, D)
```

```python
from contextlib import ExitStack

import concourse.bass as bass
from concourse import mybir

F32 = mybir.dt.float32
F32R = mybir.dt.float32r
I32 = mybir.dt.int32
ALU = mybir.AluOpType
ACT = mybir.ActivationFunctionType
AX = mybir.AxisListType.X

P = 128
NSEQ = 64
LEN = 64
D = 512
KD = D // P
BN = 256
KB = BN // P
ROLES = 3
HID = 4 * D
CH = HID // D
GS = 8
NG = NSEQ // GS + ROLES - 1
SLOTS = NG * GS
GT = GS * LEN // P
SROWS = LEN // GT
NROWS = NSEQ * SROWS
SB = 4
SBT = NSEQ * LEN // SB
TT = SBT // P
NH = SBT // 512
HT = TT // NH
XP = 4
XT = TT // XP
SEQ_SB = NSEQ // SB
LN_EPS = 1e-5
SCALE = float(D) ** -0.5
WROW = KD * BN + KB * D + KB


def product(pe, out, terms):
    last = None
    for i, ((lh, ll), (rh, rl)) in enumerate(terms):
        pe.matmul(out, lh, rh, start=(i == 0), stop=False)
        pe.matmul(out, lh, rl, start=False, stop=False)
        last = pe.matmul(out, ll, rh, start=False, stop=(i == len(terms) - 1))
    return last


def route(nc, consts, roles, codes, cb2):
    tab_src, tab_dst, tab_row, target_bias, ident = consts
    with ExitStack() as ctx:
        def sb(name, shape, dt=F32):
            return ctx.enter_context(nc.sbuf_tensor(name, shape, dt))

        def sem(name):
            return ctx.enter_context(nc.semaphore(name))

        role_i = sb("role_i", [NSEQ, 1], I32)
        role_f = sb("role_f", [NSEQ, 1])
        role_c = sb("role_c", [NSEQ, 1])
        iota3 = sb("iota3", [NSEQ, ROLES])
        onehot = sb("onehot", [NSEQ, ROLES])
        before = sb("before", [NSEQ, NSEQ])
        ones = sb("ones", [NSEQ, NSEQ])
        up_i = sb("up_i", [NSEQ, ROLES], I32)
        up_r = sb("up_r", [NSEQ, ROLES], I32)
        base = sb("base", [NSEQ, ROLES])
        place = sb("place", [NSEQ, ROLES])
        placed = sb("placed", [NSEQ, ROLES])
        slot = sb("slot", [NSEQ, 1])
        iota_slot = sb("iota_slot", [NSEQ, SLOTS])
        at_slot = sb("at_slot", [NSEQ, SLOTS])
        off_slot = sb("off_slot", [NSEQ, SLOTS])
        at_row = sb("at_row", [NSEQ, SLOTS, SROWS])
        rows = sb("rows", [P, NG])
        slot_rows = sb("slot_rows", [P, NG])
        seq_off = sb("seq_off", [NSEQ, 1])
        iota_grp = sb("iota_grp", [1, NG])
        past1 = sb("past1", [1, NG])
        past2 = sb("past2", [1, NG])
        role_at = sb("role_at", [1, NG])
        codes_i = sb("codes_i", [P, NSEQ], I32)
        codes_f = sb("codes_f", [P, NSEQ])
        feat = sb("feat", [P, KD])
        cb2_sb = sb("cb2_sb", [P, KD])
        ps_rank = ctx.enter_context(nc.psum_tensor("ps_rank", [NSEQ, 512], F32))
        ps_slot = ctx.enter_context(nc.psum_tensor("ps_slot", [P, 512], F32))

        small_in = sem("r_small_in")
        made = sem("r_made")
        dve = sem("r_dve")
        ranks = sem("r_ranks")
        slots = sem("r_slots")

        block = ctx.enter_context(nc.Block())

        @block.sync
        def _(sp):
            sp.dma_start(role_i[:], roles).then_inc(small_in, 16)
            sp.dma_start(codes_i[:], codes.broadcast_to([P, NSEQ])).then_inc(small_in, 16)
            sp.dma_start(cb2_sb[:], cb2).then_inc(small_in, 16)

        @block.gpsimd
        def _(pool):
            pool.memset(ident[:], 0.0).then_inc(made, 1)
            pool.memset(before[:], 1.0).then_inc(made, 1)
            pool.memset(ones[:], 1.0).then_inc(made, 1)
            pool.iota(iota3[:], pattern=[[1, ROLES]], base=0, channel_multiplier=0,
                      allow_small_or_imprecise_dtypes=True).then_inc(made, 1)
            pool.iota(iota_slot[:], pattern=[[1, SLOTS]], base=0, channel_multiplier=0,
                      allow_small_or_imprecise_dtypes=True).then_inc(made, 1)
            pool.iota(iota_grp[:], pattern=[[GS, NG]], base=0, channel_multiplier=0,
                      allow_small_or_imprecise_dtypes=True).then_inc(made, 1)
            pool.iota(seq_off[:], pattern=[[0, 1]], base=-NSEQ, channel_multiplier=1,
                      allow_small_or_imprecise_dtypes=True).then_inc(made, 1)
            pool.iota(feat[:], pattern=[[P, KD]], base=0, channel_multiplier=1,
                      allow_small_or_imprecise_dtypes=True).then_inc(made, 1)
            pool.iota(slot_rows[:], pattern=[[P, NG]], base=NROWS, channel_multiplier=1,
                      allow_small_or_imprecise_dtypes=True).then_inc(made, 1)
            pool.wait_ge(made, 9)
            pool.affine_select(out=ident[:], in_=ident[:], compare_op=ALU.not_equal, fill=1.0,
                               base=0, pattern=[[-1, P]], channel_multiplier=1).then_inc(made, 1)
            pool.affine_select(out=before[:], in_=before[:], compare_op=ALU.is_gt, fill=0.0,
                               base=0, pattern=[[1, NSEQ]], channel_multiplier=-1).then_inc(made, 1)

        @block.vector
        def _(v):
            steps = [0]

            def step(ins):
                ins.then_inc(dve, 1)
                steps[0] += 1
                v.wait_ge(dve, steps[0])

            v.wait_ge(small_in, 48)
            v.wait_ge(made, 11)
            step(v.tensor_copy(role_f[:], role_i[:]))
            step(v.tensor_scalar(role_c[:], role_f[:], 0.0, float(ROLES - 1), ALU.max, ALU.min))
            step(v.tensor_scalar(onehot[:], iota3[:], role_c[:], None, ALU.is_equal))
            step(v.tensor_copy(codes_f[:], codes_i[:]))
            for m in range(KD):
                step(v.tensor_scalar(target_bias[:, m, :], codes_f[:], feat[:, m:m + 1],
                                     cb2_sb[:, m:m + 1], ALU.is_equal, ALU.add))
            v.wait_ge(ranks, 1)
            step(v.tensor_scalar(up_i[:], ps_rank[:, ROLES:2 * ROLES], float(GS - 1), None, ALU.add))
            step(v.tensor_scalar(up_r[:], up_i[:], -GS, None, ALU.bitwise_and))
            step(v.memset(base[:], 0.0))
            step(v.tensor_copy(base[:, 1:2], up_r[:, 0:1]))
            step(v.tensor_tensor(base[:, 2:3], base[:, 1:2], up_r[:, 1:2], ALU.add))
            step(v.tensor_tensor(place[:], base[:], ps_rank[:, 0:ROLES], ALU.add))
            step(v.tensor_tensor(placed[:], place[:], onehot[:], ALU.mult))
            step(v.reduce_sum(slot[:], placed[:], axis=AX))
            step(v.tensor_scalar(off_slot[:], iota_slot[:], -1.0, seq_off[:], ALU.mult, ALU.add))
            step(v.scalar_tensor_tensor(out=at_slot[:], in0=iota_slot[:], scalar=slot[:], in1=off_slot[:],
                                        op0=ALU.is_equal, op1=ALU.mult))
            step(v.tensor_copy(at_row[:], at_slot[:].rearrange("b (s a) -> b s a", a=1)
                               .broadcast_to([NSEQ, SLOTS, SROWS])))
            assert steps[0] == 19
            step(v.tensor_scalar(past1[:], iota_grp[:], base[0:1, 1:2], None, ALU.is_ge))
            step(v.tensor_scalar(past2[:], iota_grp[:], base[0:1, 2:3], None, ALU.is_ge))
            step(v.tensor_tensor(role_at[:], past1[:], past2[:], ALU.add))
            for layer in range(3):
                step(v.tensor_scalar(tab_row[:, layer * NG:(layer + 1) * NG], role_at[:],
                                     float(ROLES * layer), None, ALU.add))
            v.wait_ge(slots, 1)
            step(v.scalar_tensor_tensor(out=rows[:], in0=ps_slot[:, 0:NG], scalar=float(SROWS),
                                        in1=slot_rows[:], op0=ALU.mult, op1=ALU.add))
            step(v.tensor_copy(tab_dst[:, NG:2 * NG], rows[:]))
            for half in range(2):
                step(v.tensor_scalar(tab_src[:, half * NG:(half + 1) * NG], rows[:], float(NROWS - 1), None, ALU.min))
            step(v.tensor_copy(tab_dst[:, 0:NG], rows[:]))

        @block.tensor
        def _(pe):
            pe.wait_ge(made, 11)
            pe.wait_ge(dve, 3)
            pe.matmul(ps_rank[:, 0:ROLES], before[:], onehot[:], start=True, stop=True)
            pe.matmul(ps_rank[:, ROLES:2 * ROLES], ones[:], onehot[:], start=True, stop=True)\
                .then_inc(ranks, 1)
            pe.wait_ge(dve, 19)
            for n in range(NG):
                last = pe.matmul(ps_slot[:, n:n + 1], at_row[:, n * GS:(n + 1) * GS, :].rearrange("b s r -> b (s r)"),
                                 ones[:, 0:1], start=True, stop=True)
            last.then_inc(slots, 1)


def ffn_layers(nc, tag, consts, layers, src, mid, dst, w_packed, rows_packed, w_raw, fold=None):
    tab_src, tab_dst, tab_row, _, ident = consts
    NJ = NG * len(layers)
    with ExitStack() as ctx:
        def sb(name, shape, dt=F32):
            return ctx.enter_context(nc.sbuf_tensor(f"{tag}_{name}", shape, dt))

        def pair(name, shape, dt=F32):
            return [sb(f"{name}{u}", shape, dt) for u in range(2)]

        def sem(name):
            return ctx.enter_context(nc.semaphore(f"{tag}_{name}"))

        src_row = pair("src_row", [P, 1], I32)
        dst_row = pair("dst_row", [P, 1], I32)
        row_ready = sem("row_ready")
        out_row_ready = sem("out_row_ready")
        x_tok = pair("x_tok", [P, GT, D])
        x_bias = pair("x_bias", [P, GT, D])
        xT_hi = sb("xT_hi", [P, KD, 512], F32R)
        xT_lo = sb("xT_lo", [P, KD, 512], F32R)
        wd_hi = pair("wd_hi", [P, KD, BN], F32R)
        wd_lo = pair("wd_lo", [P, KD, BN], F32R)
        wu_hi = pair("wu_hi", [P, KB, D], F32R)
        wu_lo = pair("wu_lo", [P, KB, D], F32R)
        bias_down = pair("bias_down", [P, KB])
        bias_up = pair("bias_up", [P, D])
        gain = pair("gain", [P, 2, D])
        g = pair("g", [P, 512])
        h_hi = pair("h_hi", [P, KB, 512], F32R)
        h_lo = pair("h_lo", [P, KB, 512], F32R)
        y = pair("y", [P, GT, D])
        normed = pair("normed", [P, GT, D])
        stats = sb("stats", [P, GT, 6])
        mean_var = sb("mean_var", [P, GT, 2])
        var_eps = pair("var_eps", [P, GT])
        neg_mean = pair("neg_mean", [P, GT])
        power = sb("power", [P, GT])
        rstd = pair("rstd", [P, GT])
        shift = pair("shift", [P, GT])
        bank = [ctx.enter_context(nc.psum_tensor(f"{tag}_bank{i}", [P, 512], F32)) for i in range(8)]
        bank_T, bank_D, bank_U = bank[0:4], bank[4:6], bank[6:8]

        x_in = [sem(f"x_in{u}") for u in range(2)]
        w_in = [sem(f"w_in{u}") for u in range(2)]
        bup_in = [sem(f"bup_in{u}") for u in range(2)]
        gain_in = [sem(f"gain_in{u}") for u in range(2)]
        stored = [sem(f"stored{u}") for u in range(2)]
        tr_done = sem("tr_done")
        down_done = sem("down_done")
        up_done = sem("up_done")
        xhi_done = sem("xhi_done")
        xlo_done = sem("xlo_done")
        gelu_done = sem("gelu_done")
        hhi_done = sem("hhi_done")
        hlo_done = sem("hlo_done")
        wdhi_done = sem("wdhi_done")
        wuhi_done = sem("wuhi_done")
        wdlo_done = sem("wdlo_done")
        wulo_done = sem("wulo_done")
        xb_done = sem("xb_done")
        y_done = sem("y_done")
        bn_done = sem("bn_done")
        aggr_done = sem("aggr_done")
        met = sem("met")
        const_ready = sem("const_ready")
        moments_done = sem("moments_done")
        rstd_done = sem("rstd_done")
        norm_done = sem("norm_done")
        mul_done = sem("mul_done")
        add_done = sem("add_done")
        fold_mm = sem("fold_mm")

        def steps(eng, step):
            for j in range(4):
                step(j, j // 2, j % 2)
            with eng.Fori(2, NJ // 2 - 1) as h:
                step(2 * h, h, 0)
                step(2 * h + 1, h, 1)
            step(NJ - 2, NJ // 2 - 1, 0)
            step(NJ - 1, NJ // 2 - 1, 1)

        def is_int(j, *values):
            return isinstance(j, int) and j in values

        def settled(eng):
            eng.sem_inc(met, 1)

        block = ctx.enter_context(nc.Block())

        @block.sync
        def _(sp):
            def row_of(j):
                return sp.value_load(tab_row[0:1, bass.ds(j + NG * layers[0], 1)], min_val=0, max_val=3 * ROLES - 1)

            def load(j, h, u):
                row = row_of(j)
                sp.dma_start(w_raw[u][:], w_packed[bass.ds(row, 1)].rearrange("a p n -> (a p) n")).then_inc(w_in[u], 16)
                sp.dma_start(bias_up[u][:], rows_packed[bass.ds(row, 1), 0, :].broadcast_to([P, D])).then_inc(bup_in[u], 16)

            def load_gain(j, h, u):
                sp.dma_start(gain[u][:].rearrange("p a n -> p (a n)"),
                             rows_packed[bass.ds(row_of(j), 1), 1:3, :].rearrange("r a n -> r (a n)").broadcast_to([P, 2 * D]))\
                  .then_inc(gain_in[u], 16)

            load(0, 0, 0)
            load(1, 0, 1)
            ahead_steps = (1, 2, 3, NJ - 2, NJ - 1)

            def step(j, h, u):
                if not is_int(j, NJ - 2, NJ - 1):
                    sp.wait_ge(xb_done, j + 1)
                    sp.wait_ge(wdlo_done, j + 1)
                    sp.wait_ge(wdhi_done, 2 * j + 2)
                    sp.wait_ge(wulo_done, j + 1)
                    settled(sp)
                    load(j + 2, h + 1, u)
                if not is_int(j, 0, 1):
                    sp.wait_ge(add_done, GT * j - GT)
                    settled(sp)
                load_gain(j, h, u)
                if fold and is_int(j, *ahead_steps):
                    to, of, loaded = fold[0][ahead_steps.index(j)]
                    sp.dma_start(to, of).then_inc(loaded, 16)
            steps(sp, step)

        @block.tensor
        def _(pe):
            def transposes(j, h, u):
                pe.wait_ge(x_in[u], 16 * (h + 1))
                for t in range(GT):
                    if not is_int(j, 0):
                        pe.wait_ge(xlo_done, GT * j - GT + t + 1)
                    for k in range(KD):
                        last = pe.transpose(bank_T[t][:, k * P:(k + 1) * P],
                                            x_tok[u][:, t, k * P:(k + 1) * P], ident[:])
                    last.then_inc(tr_done, 1)

            def down(j, h, u):
                pe.wait_ge(xlo_done, GT * j + GT)
                pe.wait_ge(wdlo_done, j + 1)
                for m in range(KB):
                    if not is_int(j, 0):
                        pe.wait_ge(gelu_done, KB * j - KB + m + 1)
                    ms = slice(m * P, (m + 1) * P)
                    product(pe, bank_D[m][:], [((wd_hi[u][:, k, ms], wd_lo[u][:, k, ms]),
                                                (xT_hi[:, k, :], xT_lo[:, k, :])) for k in range(KD)])\
                        .then_inc(down_done, 1)

            def up(j, h, u):
                pe.wait_ge(hlo_done, KB * j + KB)
                pe.wait_ge(wulo_done, j + 1)
                for t in range(GT):
                    if not (is_int(j, 0) and t < 2):
                        pe.wait_ge(y_done, GT * j + t - 1)
                    ts = slice(t * P, (t + 1) * P)
                    product(pe, bank_U[t % 2][:], [((h_hi[u][:, k, ts], h_lo[u][:, k, ts]),
                                                    (wu_hi[u][:, k, :], wu_lo[u][:, k, :])) for k in range(KB)])\
                        .then_inc(up_done, 1)

            def fold_tiles(f, tiles):
                _, pairs, fold_in, raw_in = fold
                left, right = pairs[f]
                pe.wait_ge(fold_in[f], 32)
                for m in tiles:
                    if f:
                        pe.wait_ge(raw_in[0], 16 // KD * (m + 1))
                    for k in range(KD):
                        last = pe.matmul(bank_T[m][:], left[:, k * D + m * P:k * D + (m + 1) * P],
                                         right[:, k * D:(k + 1) * D], start=(k == 0), stop=(k == KD - 1))
                    last.then_inc(fold_mm, 1)

            transposes(0, 0, 0)

            def step(j, h, u):
                down(j, h, u)
                if not is_int(j, NJ - 1):
                    transposes(j + 1, h + u, 1 - u)
                elif fold:
                    fold_tiles(0, range(KD // 2))
                if not is_int(j, 0):
                    up(j - 1, h - 1 + u, 1 - u)
                if fold and is_int(j, NJ - 1):
                    fold_tiles(0, range(KD // 2, KD))
            steps(pe, step)
            up(NJ - 1, NJ // 2 - 1, 1)
            if fold:
                fold_tiles(1, range(KD))

        @block.scalar
        def _(act):
            def split_down(j, h, u):
                act.wait_ge(w_in[u], 16 * (h + 1))
                act.activation(wd_hi[u][:].rearrange("p k n -> p (k n)"), w_raw[u][:, 0:KD * BN], ACT.Copy).then_inc(wdhi_done, 1)
                act.activation(bias_down[u][:], w_raw[u][:, KD * BN + KB * D:WROW], ACT.Copy).then_inc(wdhi_done, 1)

            def split_up(j, h, u):
                if not is_int(j, 0, 1):
                    act.wait_ge(up_done, GT * j - GT)
                act.activation(wu_hi[u][:].rearrange("p k n -> p (k n)"),
                               w_raw[u][:, KD * BN:KD * BN + KB * D], ACT.Copy).then_inc(wuhi_done, 1)

            def transposed_hi(j, h, u):
                for t in range(GT):
                    act.wait_ge(tr_done, GT * j + t + 1)
                    act.activation(xT_hi[:, :, t * P:(t + 1) * P],
                                   bank_T[t][:].rearrange("p (k t) -> p k t", k=KD), ACT.Copy).then_inc(xhi_done, 1)

            def gelu(j, h, u):
                act.wait_ge(wdhi_done, 2 * j + 2)
                for m in range(KB):
                    act.wait_ge(down_done, KB * j + m + 1)
                    if not is_int(j, 0):
                        act.wait_ge(hlo_done, KB * j - KB + m + 1)
                    act.activation(g[m][:], bank_D[m][:], ACT.Gelu, bias=bias_down[u][:, m:m + 1]).then_inc(gelu_done, 1)
                    act.wait_ge(gelu_done, KB * j + m + 1)
                    act.activation(h_hi[u][:, m, :], g[m][:], ACT.Copy).then_inc(hhi_done, 1)

            def norm(j, h, u):
                act.wait_ge(rstd_done, 2 * j + 2)
                for t in range(GT):
                    act.activation(y[u][:, t, :], y[u][:, t, :], ACT.Identity,
                                   scale=rstd[u][:, t:t + 1], bias=shift[u][:, t:t + 1]).then_inc(norm_done, 1)

            def folded(f):
                for m in range(KD):
                    act.wait_ge(fold_mm, KD * f + m + 1)
                    act.activation(w_raw[f][:, m * D:(m + 1) * D], bank_T[m][:], ACT.Copy).then_inc(fold[3][f], 16 // KD)

            split_down(0, 0, 0)
            transposed_hi(0, 0, 0)

            def step(j, h, u):
                split_up(j, h, u)
                gelu(j, h, u)
                if not is_int(j, NJ - 1):
                    split_down(j + 1, h + u, 1 - u)
                    transposed_hi(j + 1, h + u, 1 - u)
                if not is_int(j, 0, 1):
                    norm(j - 2, h - 1, u)
            steps(act, step)
            norm(NJ - 2, NJ // 2 - 1, 0)
            if fold:
                act.wait_ge(wdlo_done, NJ)
                act.wait_ge(wulo_done, NJ)
                folded(0)
            norm(NJ - 1, NJ // 2 - 1, 1)
            if fold:
                folded(1)

        @block.vector
        def _(v):
            def split_down(j, h, u):
                v.wait_ge(wdhi_done, 2 * j + 1)
                v.tensor_tensor(wd_lo[u][:].rearrange("p k n -> p (k n)"), w_raw[u][:, 0:KD * BN],
                                wd_hi[u][:].bitcast(F32).rearrange("p k n -> p (k n)"), ALU.subtract).then_inc(wdlo_done, 1)

            def split_up(j, h, u):
                v.wait_ge(wuhi_done, j + 1)
                v.tensor_tensor(wu_lo[u][:].rearrange("p k n -> p (k n)"), w_raw[u][:, KD * BN:KD * BN + KB * D],
                                   wu_hi[u][:].bitcast(F32).rearrange("p k n -> p (k n)"), ALU.subtract).then_inc(wulo_done, 1)

            def transposed_lo(j, h, u, t):
                v.wait_ge(xhi_done, GT * j + t + 1)
                v.tensor_tensor(xT_lo[:, :, t * P:(t + 1) * P], bank_T[t][:].rearrange("p (k t) -> p k t", k=KD),
                                xT_hi[:, :, t * P:(t + 1) * P].bitcast(F32), ALU.subtract).then_inc(xlo_done, 1)

            def hidden_lo(j, h, u, m):
                v.wait_ge(hhi_done, KB * j + m + 1)
                v.tensor_tensor(h_lo[u][:, m, :], g[m][:], h_hi[u][:, m, :].bitcast(F32), ALU.subtract).then_inc(hlo_done, 1)

            def shift_gain(j, h, u, t):
                v.wait_ge(mul_done, GT * j + t + 1)
                v.tensor_tensor(normed[u][:, t, :], normed[u][:, t, :], gain[u][:, 1, :], ALU.add).then_inc(add_done, 1)

            def residual(j, h, u, t):
                if t == 0:
                    v.wait_ge(xb_done, j + 1)
                    if not is_int(j, 0, 1):
                        v.wait_ge(mul_done, GT * j - GT)
                v.wait_ge(up_done, GT * j + t + 1)
                v.tensor_tensor(y[u][:, t, :], bank_U[t % 2][:], x_bias[u][:, t, :], ALU.add).then_inc(y_done, 1)

            def statistics(j, h, u, t):
                v.wait_ge(y_done, GT * j + t + 1)
                v.bn_stats(stats[:, t, :], y[u][:, t, :]).then_inc(bn_done, 1)

            def aggregate(j, h, u):
                v.wait_ge(bn_done, GT * j + GT)
                settled(v)
                for t in range(GT):
                    v.bn_aggr(mean_var[:, t, :], stats[:, t, :]).then_inc(aggr_done, 1)
                if not is_int(j, 0, 1):
                    v.wait_ge(rstd_done, 2 * j - 2)
                v.wait_ge(aggr_done, GT * j + GT)
                v.tensor_scalar(var_eps[u][:], mean_var[:, :, 1], LN_EPS, None, ALU.add).then_inc(moments_done, 1)
                v.tensor_scalar(neg_mean[u][:], mean_var[:, :, 0], -1.0, None, ALU.mult).then_inc(moments_done, 1)

            split_down(0, 0, 0)
            for t in range(GT):
                transposed_lo(0, 0, 0, t)

            def step(j, h, u):
                hidden_lo(j, h, u, 0)
                split_up(j, h, u)
                hidden_lo(j, h, u, 1)
                if not is_int(j, NJ - 1):
                    split_down(j + 1, h + u, 1 - u)
                for t in range(GT):
                    if not is_int(j, NJ - 1):
                        transposed_lo(j + 1, h + u, 1 - u, t)
                    if not is_int(j, 0) and 1 <= t <= 2:
                        residual(j - 1, h - 1 + u, 1 - u, t - 1)
                for t in range(GT):
                    if not is_int(j, 0):
                        statistics(j - 1, h - 1 + u, 1 - u, t)
                        if t < GT - 2:
                            residual(j - 1, h - 1 + u, 1 - u, t + 2)
                    if not is_int(j, 0, 1):
                        shift_gain(j - 2, h - 1, u, t)
                if not is_int(j, 0):
                    aggregate(j - 1, h - 1 + u, 1 - u)
            steps(v, step)
            for t in range(GT):
                residual(NJ - 1, NJ // 2 - 1, 1, t)
                shift_gain(NJ - 2, NJ // 2 - 1, 0, t)
                statistics(NJ - 1, NJ // 2 - 1, 1, t)
            aggregate(NJ - 1, NJ // 2 - 1, 1)
            for t in range(GT):
                shift_gain(NJ - 1, NJ // 2 - 1, 1, t)

        @block.gpsimd
        def _(pool):
            def add_bias(j, h, u):
                pool.wait_ge(x_in[u], 16 * (h + 1))
                pool.wait_ge(bup_in[u], 16 * (h + 1))
                if not is_int(j, 0, 1):
                    pool.wait_ge(y_done, GT * j - GT)
                pool.tensor_tensor(x_bias[u][:], x_tok[u][:],
                                   bias_up[u][:].rearrange("p (a n) -> p a n", a=1).broadcast_to([P, GT, D]),
                                   ALU.add).then_inc(xb_done, 1)

            def rstd_shift(j, h, u):
                pool.wait_ge(const_ready, 1)
                pool.wait_ge(moments_done, 2 * j + 2)
                pool.tensor_tensor(rstd[u][:], var_eps[u][:], power[:], ALU.pow).then_inc(rstd_done, 1)
                pool.wait_ge(rstd_done, 2 * j + 1)
                pool.tensor_tensor(shift[u][:], neg_mean[u][:], rstd[u][:], ALU.mult).then_inc(rstd_done, 1)

            def multiply_gain(j, h, u):
                pool.wait_ge(gain_in[u], 16 * (h + 1))
                if not is_int(j, 0, 1):
                    pool.wait_ge(stored[u], 16 * h)
                for t in range(GT):
                    pool.wait_ge(norm_done, GT * j + t + 1)
                    pool.tensor_tensor(normed[u][:, t, :], y[u][:, t, :], gain[u][:, 0, :], ALU.mult).then_inc(mul_done, 1)

            def either(j, first, second):
                if len(layers) == 1:
                    first()
                elif isinstance(j, int):
                    (first if j < NG else second)()
                else:
                    with pool.If(j < NG):
                        first()
                    with pool.Else():
                        second()

            def gather(j, h, u):
                pool.tensor_copy(src_row[u][:], tab_src[:, bass.ds(j, 1)]).then_inc(row_ready, 1)
                pool.wait_ge(row_ready, j + 1)
                settled(pool)
                to = x_tok[u][:].rearrange("p t n -> p (t n)")

                def sequences():
                    pool.indirect_dma_start(out=to, out_offset=None, in_=src,
                                            in_offset=bass.IndirectOffsetOnAxis(ap=src_row[u][:], axis=0)).then_inc(x_in[u], 16)

                def first_layers():
                    pool.dma_start(to, mid[bass.ds(j * P, P), :]).then_inc(x_in[u], 16)
                either(j, sequences, first_layers)

            def scatter(j, h, u):
                pool.wait_ge(add_done, GT * j + GT)
                pool.tensor_copy(dst_row[u][:], tab_dst[:, bass.ds(j + NG * (2 - len(layers)), 1)]).then_inc(out_row_ready, 1)
                pool.wait_ge(out_row_ready, j + 1)
                settled(pool)
                of = normed[u][:].rearrange("p t n -> p (t n)")

                def first_layers():
                    pool.dma_start(mid[bass.ds((j + NG) * P, P), :], of).then_inc(stored[u], 16)

                def sequences():
                    pool.indirect_dma_start(out=dst, out_offset=bass.IndirectOffsetOnAxis(ap=dst_row[u][:], axis=0),
                                            in_=of, in_offset=None).then_inc(stored[u], 16)
                either(j, first_layers if len(layers) > 1 else sequences, sequences)

            pool.memset(power[:], -0.5).then_inc(const_ready, 1)
            gather(0, 0, 0)
            gather(1, 0, 1)

            def step(j, h, u):
                add_bias(j, h, u)
                if not is_int(j, NJ - 2, NJ - 1):
                    pool.wait_ge(tr_done, GT * j + GT)
                    pool.wait_ge(xb_done, j + 1)
                    gather(j + 2, h + 1, u)
                if not is_int(j, 0, 1):
                    multiply_gain(j - 2, h - 1, u)
                    scatter(j - 2, h - 1, u)
                if not is_int(j, 0):
                    rstd_shift(j - 1, h - 1 + u, 1 - u)
            steps(pool, step)
            multiply_gain(NJ - 2, NJ // 2 - 1, 0)
            scatter(NJ - 2, NJ // 2 - 1, 0)
            rstd_shift(NJ - 1, NJ // 2 - 1, 1)
            multiply_gain(NJ - 1, NJ // 2 - 1, 1)
            scatter(NJ - 1, NJ // 2 - 1, 1)
            for u in range(2):
                pool.wait_ge(stored[u], 16 * (NJ // 2))


def core_layer(nc, consts, early, units_a, units_b, units_c, fold_m, fold_v, bias_cols, src, dst):
    _, _, _, target_bias, ident = consts
    w_rows, first_c, places, raw_in = early
    w_raw = [w[:, 0:KD * D] for w in w_rows]
    NA, NBU, NC = 2 * CH + 1, 2 * CH + 1, CH
    TILES = KD * NH
    HTILES = 2 * CH * TILES
    with ExitStack() as ctx:
        place = [nc.sbuf_base]

        def sb(name, shape, dt=F32, at=None):
            size = 1
            for x in shape[1:]:
                size *= x
            if at is None:
                at = (place[0] + 31) // 32 * 32
                place[0] = at + 4 * size
                where[name] = at
            return nc.alloc_sbuf_tensor_at(name, shape, dt, offset=at)

        where = {}

        def sem(name):
            return ctx.enter_context(nc.semaphore(name))

        x_tok = sb("x_tok", [P, TT, D])
        base = x_tok[:].rearrange("p t n -> p (t n)")
        cms = base.rearrange("p (k n) -> p k n", k=KD)
        acc = sb("acc", [P, KD, SBT])
        xc_hi = sb("xc_hi", [P, KD, SBT], F32R)
        xc_lo = sb("xc_lo", [P, KD, SBT], F32R)
        o_hi = sb("o_hi", [P, KD, SBT], F32R, at=places["o_hi"])
        o_lo = sb("o_lo", [P, KD, SBT], F32R, at=places["o_lo"])
        h_hi = sb("h_hi", [P, KD, SBT], F32R)
        h_lo = sb("h_lo", [P, KD, SBT], F32R)
        a_hi = h_hi[:].rearrange("p k n -> p (k n)")[:, 0:KD * 512].rearrange("p (k n) -> p k n", k=KD)
        a_lo = h_lo[:].rearrange("p k n -> p (k n)")[:, 0:KD * 512].rearrange("p (k n) -> p k n", k=KD)
        yT = sb("yT", [P, KD, 512], at=where["h_hi"] + 4 * KD * 512)
        stage = sb("stage", [P, TT, D], at=where["h_lo"])
        w_hi = {s: sb(f"w_hi{s}", [P, KD, D], F32R) for s in "ABC"}
        w_lo = {s: sb(f"w_lo{s}", [P, KD, D], F32R, at=places["first_c"] if s == "C" else None) for s in "ABC"}
        g = [sb(f"g{i}", [P, 512]) for i in range(2)]
        probs = sb("probs", [P, HT, P])
        probsT = sb("probsT", [P, HT, P])
        row_max = sb("row_max", [P, HT])
        row_sum = sb("row_sum", [P, HT])
        row_inv = sb("row_inv", [P, HT])
        expd = sb("expd", [P, HT, LEN])
        bias = sb("bias_cols", [P, 2 * HID // P + 2 * KD])
        cb1, mb1 = bias[:, 0:HID // P], bias[:, HID // P:2 * HID // P]
        bp, mb2 = bias[:, 2 * HID // P:2 * HID // P + KD], bias[:, 2 * HID // P + KD:]
        bank = [ctx.enter_context(nc.psum_tensor(f"bank{i}", [P, 512], F32)) for i in range(8)]

        x_in = [sem(f"x_in{i}") for i in range(XP)]
        bias_in = sem("bias_in")
        stored = [sem(f"stored{i}") for i in range(2)]
        hi_done = {s: sem(f"hi_done{s}") for s in "ABC"}
        lo_done = {s: sem(f"lo_done{s}") for s in "ABC"}
        tr_done = sem("tr_done")
        xraw_done = sem("xraw_done")
        xhi_done = sem("xhi_done")
        xlo_done = sem("xlo_done")
        y_mm = sem("y_mm")
        y_done = sem("y_done")
        s_mm = sem("s_mm")
        max_done = sem("max_done")
        sub_done = sem("sub_done")
        exp_done = sem("exp_done")
        sum_done = sem("sum_done")
        inv_done = sem("inv_done")
        zeroed = sem("zeroed")
        probs_done = sem("probs_done")
        pt_mm = sem("pt_mm")
        pt_done = sem("pt_done")
        av_mm = sem("av_mm")
        ahi_done = sem("ahi_done")
        alo_done = sem("alo_done")
        o_mm = sem("o_mm")
        ohi_done = sem("ohi_done")
        olo_done = sem("olo_done")
        init_done = sem("init_done")
        hid_mm = sem("hid_mm")
        gelu_done = sem("gelu_done")
        hhi_done = sem("hhi_done")
        hlo_done = sem("hlo_done")
        out_mm = sem("out_mm")
        acc_done = sem("acc_done")
        chi_done = sem("chi_done")
        clo_done = sem("clo_done")
        sum_ready = sem("sum_ready")
        fin_mm = sem("fin_mm")
        fold_stored = sem("fold_stored")
        fin_done = sem("fin_done")
        met = sem("met")

        def settled(eng):
            eng.sem_inc(met, 1)

        def cols(n):
            return slice(n * 512, (n + 1) * 512)

        block = ctx.enter_context(nc.Block())

        @block.sync
        def _(sp):
            def load_a(s, k, unit):
                sp.wait_ge(lo_done["A"], NA * s + k)
                sp.dma_start(w_raw[0], unit).then_inc(raw_in[0], 16)

            def load_bc(s, before_b, before_c, unit):
                sp.wait_ge(lo_done["B"], NBU * s + before_b)
                settled(sp)
                sp.wait_ge(lo_done["C"], NC * s + before_c)
                sp.dma_start(w_raw[1], unit).then_inc(raw_in[1], 16)

            def load_x(s):
                for i in range(XP):
                    sp.dma_start(x_tok[:, i * XT:(i + 1) * XT, :], src[bass.ds(s * SBT + i * XT * P, XT * P), :]
                                 .rearrange("(t p) n -> p t n", p=P)).then_inc(x_in[i], 16)

            sp.dma_start(bias[:], bias_cols).then_inc(bias_in, 16)
            load_x(0)
            for i, to in enumerate((fold_m, fold_v)):
                sp.wait_ge(raw_in[i], 16)
                sp.dma_start(to, w_raw[i]).then_inc(fold_stored, 16)
            sp.wait_ge(fold_stored, 32)

            def super_block(s, more):
                load_a(s, 1, units_a[0])
                load_bc(s, 1, 1, units_b[0])
                for c in range(CH):
                    load_a(s, 2 + c, units_a[1 + c])
                    load_bc(s, 2 + c, 1, units_b[1 + c])
                for c in range(CH):
                    load_a(s, 2 + CH + c, units_a[1 + CH + c] if c < CH - 1 else fold_m)
                    load_bc(s, 2 + CH + c, 1 + c, units_c[(c + 1) % CH])
                    load_bc(s, 2 + CH + c, 2 + c, units_b[1 + CH + c] if c < CH - 1 else fold_v)
                    if more and c == 0:
                        sp.wait_ge(sum_ready, TILES * s + TILES)
                        load_x(s + 1)
                for t in range(TT):
                    sp.wait_ge(fin_done, TT * s + TT + t + 1)
                    sp.dma_start(dst[bass.ds(s * SBT + t * P, P), :], stage[:, t, :]).then_inc(stored[t % 2], 16)
                for i in range(2):
                    sp.wait_ge(stored[i], 8 * TT * s + 8 * TT)
                    settled(sp)

            with sp.Fori(0, SB - 1) as s:
                super_block(s, True)
            super_block(SB - 1, False)

        @block.tensor
        def _(pe):
            def unit_terms(slot, m, hi, lo, n):
                ms = slice(m * P, (m + 1) * P)
                return [((w_hi[slot][:, k, ms], w_lo[slot][:, k, ms]), (hi[:, k, cols(n)], lo[:, k, cols(n)]))
                        for k in range(KD)]

            def super_block(s):
                for t in range(TT):
                    if t % XT == 0:
                        pe.wait_ge(x_in[t // XT], 16 * s + 16)
                    pe.wait_ge(fin_done, TT * s + t + 1)
                    for k in range(KD):
                        last = pe.transpose(bank[t][:, k * P:(k + 1) * P], x_tok[:, t, k * P:(k + 1) * P], ident[:])
                    last.then_inc(tr_done, 1)

                def query(n):
                    pe.wait_ge(xlo_done, TT * s + HT * (n + 1))
                    for m in range(KD):
                        product(pe, bank[m][:], unit_terms("A", m, xc_hi, xc_lo, n)).then_inc(y_mm, 1)

                def scores(n):
                    pe.wait_ge(y_done, TILES * s + KD * (n + 1))
                    if n == 0:
                        pe.wait_ge(xlo_done, TT * s + HT + 1)
                    for i in range(HT):
                        t = HT * n + i
                        for k in range(KD):
                            last = pe.matmul(bank[4 + n][:, i * P:(i + 1) * P], yT[:, k, i * P:(i + 1) * P],
                                             acc[:, k, t * P:(t + 1) * P], start=(k == 0), stop=(k == KD - 1))
                    last.then_inc(s_mm, 1)

                def turn_probs(n):
                    pe.wait_ge(probs_done, 2 * NH * s + 2 * (n + 1))
                    for i in range(HT):
                        last = pe.transpose(bank[6 + n][:, i * P:(i + 1) * P], probs[:, i, :], ident[:])
                    last.then_inc(pt_mm, 1)

                def attend(n):
                    pe.wait_ge(pt_done, NH * s + n + 1)
                    for i in range(HT):
                        for k in range(KD):
                            last = pe.matmul(bank[i][:, k * P:(k + 1) * P], x_tok[:, HT * n + i, k * P:(k + 1) * P],
                                             probsT[:, i, :], start=True, stop=True)
                        last.then_inc(av_mm, 1)

                def output(n):
                    pe.wait_ge(alo_done, TT * s + HT * (n + 1))
                    for m in range(KD):
                        if n or m >= 2:
                            pe.wait_ge(olo_done, TILES * s + KD * n + m - 1)
                        ms = slice(m * P, (m + 1) * P)
                        product(pe, bank[4 + 2 * (m % 2)][:],
                                [((w_hi["B"][:, k, ms], w_lo["B"][:, k, ms]), (a_hi[:, k, :], a_lo[:, k, :]))
                                 for k in range(KD)]).then_inc(o_mm, 1)

                pe.wait_ge(lo_done["A"], NA * s + 1)
                query(0)
                scores(0)
                query(1)
                turn_probs(0)
                scores(1)
                attend(0)
                pe.wait_ge(lo_done["B"], NBU * s + 1)
                output(0)
                turn_probs(1)
                attend(1)
                output(1)

                def hidden(c, q, units):
                    n, j = q % NH, q // NH
                    if q >= 4:
                        pe.wait_ge(gelu_done, HTILES * s + TILES * c + q - 3)
                    product(pe, bank[q % 4][:], units(j, n)).then_inc(hid_mm, 1)

                def out_tiles(c, slot_b):
                    pe.wait_ge(lo_done["B"], slot_b)
                    for n in range(NH):
                        pe.wait_ge(hlo_done, HTILES * s + TILES * c + TILES - NH + 1 + n)
                        for m in range(KD):
                            r = KD * n + m
                            if r >= 4:
                                pe.wait_ge(acc_done, HTILES * s + TILES * c + r - 3)
                            product(pe, bank[4 + r % 4][:], unit_terms("B", m, h_hi, h_lo, n)).then_inc(out_mm, 1)

                with pe.Fori(0, CH) as c:
                    pe.wait_ge(lo_done["A"], NA * s + c + 2)
                    for q in range(TILES):
                        if q < NH:
                            pe.wait_ge(olo_done, TILES * s + KD * (q + 1))
                        hidden(c, q, lambda j, n: unit_terms("A", j, o_hi, o_lo, n))
                    out_tiles(c, NBU * s + c + 2)
                with pe.Fori(0, CH) as c:
                    pe.wait_ge(lo_done["A"], NA * s + c + 2 + CH)
                    pe.wait_ge(lo_done["C"], NC * s + c + 1)
                    for q in range(4):
                        n, j = q % NH, q // NH
                        for i, ((lh, ll), (rh, rl)) in enumerate(unit_terms("A", j, o_hi, o_lo, n)):
                            pe.matmul(bank[q][:], lh, rh, start=(i == 0), stop=False)
                            pe.matmul(bank[q][:], lh, rl, start=False, stop=False)
                            pe.matmul(bank[q][:], ll, rh, start=False, stop=False)
                    for q in range(4):
                        n, j = q % NH, q // NH
                        if q < NH:
                            pe.wait_ge(clo_done, TILES * s + KD * (n + 1))
                        for i, ((lh, ll), (rh, rl)) in enumerate(unit_terms("C", j, xc_hi, xc_lo, n)):
                            pe.matmul(bank[q][:], lh, rh, start=False, stop=False)
                            pe.matmul(bank[q][:], lh, rl, start=False, stop=False)
                            last = pe.matmul(bank[q][:], ll, rh, start=False, stop=(i == KD - 1))
                        last.then_inc(hid_mm, 1)
                    for q in range(4, TILES):
                        hidden(c + CH, q, lambda j, n: unit_terms("A", j, o_hi, o_lo, n)
                               + unit_terms("C", j, xc_hi, xc_lo, n))
                    out_tiles(c + CH, NBU * s + c + 2 + CH)

                for t in range(TT):
                    if t % HT == 0:
                        pe.wait_ge(acc_done, HTILES * (s + 1) - TILES + KD * (t // HT + 1))
                    for m in range(KD):
                        last = pe.transpose(bank[t][:, m * P:(m + 1) * P], acc[:, m, t * P:(t + 1) * P], ident[:])
                    last.then_inc(fin_mm, 1)

            with pe.Fori(0, SB) as s:
                super_block(s)

        @block.scalar
        def _(act):
            def split(slot, n_raw, raw=None):
                i = 0 if slot == "A" else 1
                act.wait_ge(raw_in[i], 16 * n_raw)
                act.activation(w_hi[slot][:].rearrange("p k n -> p (k n)"), w_raw[i] if raw is None else raw, ACT.Copy).then_inc(hi_done[slot], 1)

            def super_block(s):
                nb = (NBU + NC) * s
                for t in range(TT):
                    act.wait_ge(tr_done, TT * s + t + 1)
                    tile = bank[t][:].rearrange("p (k t) -> p k t", k=KD)
                    act.activation(acc[:, :, t * P:(t + 1) * P], tile, ACT.Copy).then_inc(xraw_done, 1)
                    act.activation(xc_hi[:, :, t * P:(t + 1) * P], tile, ACT.Copy).then_inc(xhi_done, 1)

                def query(n):
                    for m in range(KD):
                        act.wait_ge(y_mm, TILES * s + KD * n + m + 1)
                        act.activation(yT[:, m, :], bank[m][:], ACT.Copy).then_inc(y_done, 1)

                def softmax(n):
                    act.wait_ge(sub_done, 2 * NH * s + 2 * (n + 1))
                    act.activation(expd[:], expd[:], ACT.Exp, scale=SCALE).then_inc(exp_done, 1)

                def turned(n):
                    act.wait_ge(pt_mm, NH * s + n + 1)
                    act.activation(probsT[:].rearrange("p i t -> p (i t)"), bank[6 + n][:], ACT.Copy).then_inc(pt_done, 1)

                def attended(n):
                    for i in range(HT):
                        act.wait_ge(av_mm, TT * s + HT * n + i + 1)
                        act.activation(a_hi[:, :, i * P:(i + 1) * P], bank[i][:].rearrange("p (k t) -> p k t", k=KD),
                                       ACT.Copy).then_inc(ahi_done, 1)

                def output(n):
                    for m in range(KD):
                        act.wait_ge(o_mm, TILES * s + KD * n + m + 1)
                        act.activation(o_hi[:, m, cols(n)], bank[4 + 2 * (m % 2)][:], ACT.Identity,
                                       bias=bp[:, m:m + 1]).then_inc(ohi_done, 1)

                query(0)
                softmax(0)
                query(1)
                turned(0)
                split("A", NA * s + 2)
                attended(0)
                softmax(1)
                output(0)
                turned(1)
                attended(1)
                output(1)
                split("B", nb + 3)

                def chunk(c, bias_at):
                    for q in range(TILES):
                        n, j = q % NH, q // NH
                        at = HTILES * s + TILES * c + q + 1
                        act.wait_ge(hid_mm, at)
                        if q >= 2:
                            act.wait_ge(hlo_done, at - 2)
                        settled(act)
                        act.activation(g[q % 2][:], bank[q % 4][:], ACT.Gelu,
                                       bias=bias_at(j)).then_inc(gelu_done, 1)
                        act.wait_ge(gelu_done, at)
                        act.activation(h_hi[:, j, cols(n)], g[q % 2][:], ACT.Copy).then_inc(hhi_done, 1)

                with act.Fori(0, CH) as c:
                    chunk(c, lambda j: cb1[:, bass.ds(c * KD + j, 1)])
                    split("A", NA * s + c + 3)
                    act.wait_ge(out_mm, HTILES * s + TILES * c + TILES)
                    split("B", nb + c + 4)
                for r in range(TILES):
                    n, m = r // KD, r % KD
                    act.wait_ge(acc_done, HTILES * s + TILES * (CH - 1) + r + 1)
                    act.activation(xc_hi[:, m, cols(n)], cms[:, m, cols(n)], ACT.Copy).then_inc(chi_done, 1)
                with act.Fori(0, CH) as c:
                    chunk(c + CH, lambda j: mb1[:, bass.ds(c * KD + j, 1)])
                    split("A", NA * s + c + 3 + CH)
                    split("C", nb + 2 * c + 4 + CH)
                    act.wait_ge(out_mm, HTILES * s + TILES * (c + CH) + TILES)
                    split("B", nb + 2 * c + 5 + CH)

            act.wait_ge(bias_in, 16)
            split("A", 1)
            split("B", 2)
            split("C", 2, first_c[:])
            with act.Fori(0, SB) as s:
                super_block(s)

        @block.vector
        def _(v):
            def split(slot, n, raw=None):
                i = 0 if slot == "A" else 1
                v.wait_ge(hi_done[slot], n)
                v.tensor_tensor(w_lo[slot][:].rearrange("p k n -> p (k n)"), w_raw[i] if raw is None else raw,
                                w_hi[slot][:].bitcast(F32).rearrange("p k n -> p (k n)"), ALU.subtract).then_inc(lo_done[slot], 1)

            def super_block(s):
                for t in range(TT):
                    v.wait_ge(xhi_done, TT * s + t + 1)
                    v.tensor_tensor(xc_lo[:, :, t * P:(t + 1) * P], bank[t][:].rearrange("p (k t) -> p k t", k=KD),
                                    xc_hi[:, :, t * P:(t + 1) * P].bitcast(F32), ALU.subtract).then_inc(xlo_done, 1)

                def softmax(n):
                    v.wait_ge(s_mm, NH * s + n + 1)
                    at = NH * s + n
                    tile = bank[4 + n][:].rearrange("p (i t) -> p i t", i=HT)
                    for q in range(2):
                        ps = slice(q * LEN, (q + 1) * LEN)
                        v.reduce_max(row_max[ps, :], tile[ps, :, ps], axis=AX).then_inc(max_done, 1)
                    v.wait_ge(max_done, 2 * at + 2)
                    for q in range(2):
                        ps = slice(q * LEN, (q + 1) * LEN)
                        v.tensor_tensor(expd[ps, :, :], tile[ps, :, ps],
                                        row_max[ps, :].rearrange("p (i a) -> p i a", a=1).broadcast_to([LEN, HT, LEN]),
                                        ALU.subtract).then_inc(sub_done, 1)
                    v.wait_ge(exp_done, at + 1)
                    v.reduce_sum(row_sum[:], expd[:], axis=AX).then_inc(sum_done, 1)
                    v.wait_ge(sum_done, at + 1)
                    v.reciprocal(row_inv[:], row_sum[:]).then_inc(inv_done, 1)
                    v.wait_ge(inv_done, at + 1)
                    for q in range(2):
                        ps = slice(q * LEN, (q + 1) * LEN)
                        v.tensor_tensor(probs[ps, :, ps], expd[ps, :, :],
                                        row_inv[ps, :].rearrange("p (i a) -> p i a", a=1).broadcast_to([LEN, HT, LEN]),
                                        ALU.mult).then_inc(probs_done, 1)

                def attended(n):
                    for i in range(HT):
                        v.wait_ge(ahi_done, TT * s + HT * n + i + 1)
                        cs = slice(i * P, (i + 1) * P)
                        v.tensor_tensor(a_lo[:, :, cs], bank[i][:].rearrange("p (k t) -> p k t", k=KD),
                                        a_hi[:, :, cs].bitcast(F32), ALU.subtract).then_inc(alo_done, 1)

                def output(n):
                    for m in range(KD):
                        v.wait_ge(ohi_done, TILES * s + KD * n + m + 1)
                        v.scalar_tensor_tensor(out=o_lo[:, m, cols(n)], in0=bank[4 + 2 * (m % 2)][:],
                                               scalar=bp[:, m:m + 1], in1=o_hi[:, m, cols(n)].bitcast(F32),
                                               op0=ALU.add, op1=ALU.subtract).then_inc(olo_done, 1)

                softmax(0)
                split("A", NA * s + 2)
                attended(0)
                softmax(1)
                output(0)
                attended(1)
                output(1)
                split("B", NBU * s + 2)

                def hidden_lo(c):
                    for q in range(TILES):
                        n, j = q % NH, q // NH
                        v.wait_ge(hhi_done, HTILES * s + TILES * c + q + 1)
                        v.tensor_tensor(h_lo[:, j, cols(n)], g[q % 2][:], h_hi[:, j, cols(n)].bitcast(F32),
                                        ALU.subtract).then_inc(hlo_done, 1)

                def accumulate(c, into):
                    for r in range(TILES):
                        n, m = r // KD, r % KD
                        v.wait_ge(out_mm, HTILES * s + TILES * c + r + 1)
                        v.tensor_tensor(into[:, m, cols(n)], bank[4 + r % 4][:], into[:, m, cols(n)],
                                        ALU.add).then_inc(acc_done, 1)

                with v.Fori(0, CH) as c:
                    hidden_lo(c)
                    split("A", NA * s + c + 3)
                    v.wait_ge(init_done, KD * s + KD)
                    accumulate(c, cms)
                    split("B", NBU * s + c + 3)
                for r in range(TILES):
                    n, m = r // KD, r % KD
                    v.wait_ge(chi_done, TILES * s + r + 1)
                    v.tensor_tensor(xc_lo[:, m, cols(n)], cms[:, m, cols(n)], xc_hi[:, m, cols(n)].bitcast(F32),
                                    ALU.subtract).then_inc(clo_done, 1)
                for r in range(TILES):
                    n, m = r // KD, r % KD
                    v.scalar_tensor_tensor(out=acc[:, m, cols(n)], in0=cms[:, m, cols(n)], scalar=mb2[:, m:m + 1],
                                           in1=acc[:, m, cols(n)], op0=ALU.add, op1=ALU.add).then_inc(sum_ready, 1)
                v.wait_ge(sum_ready, TILES * s + TILES)
                settled(v)
                with v.Fori(0, CH) as c:
                    hidden_lo(c + CH)
                    split("A", NA * s + c + 3 + CH)
                    split("C", NC * s + c + 2)
                    accumulate(c + CH, acc)
                    split("B", NBU * s + c + 3 + CH)
                for t in range(TT):
                    v.wait_ge(fin_mm, TT * s + t + 1)
                    v.tensor_scalar(stage[:, t, :], bank[t][:], 0.0, 1.0, ALU.max, ALU.min).then_inc(fin_done, 1)

            v.wait_ge(bias_in, 16)
            v.wait_ge(zeroed, 1)
            v.sem_inc(fin_done, TT)
            split("A", 1)
            split("B", 1)
            split("C", 1, first_c[:])
            with v.Fori(0, SB) as s:
                super_block(s)

        @block.gpsimd
        def _(pool):
            pool.memset(probs[:], 0.0).then_inc(zeroed, 1)
            with pool.Fori(0, SB) as s:
                pool.wait_ge(av_mm, TT * s + TT)
                for m in range(KD):
                    pool.tensor_copy(cms[:, m, :].rearrange("p (b l) -> p b l", l=LEN),
                                     target_bias[:, m, bass.ds(s * SEQ_SB, SEQ_SB)]
                                     .rearrange("p (b a) -> p b a", a=1).broadcast_to([P, SEQ_SB, LEN]))\
                        .then_inc(init_done, 1)


def packed_linear(a):
    import numpy as np
    *lead, rows, n = a.shape
    a = a.reshape(*lead, rows // P, P, n)
    return np.swapaxes(a, -3, -2).reshape(*lead, P, rows // P * n)


def column_tiles(a):
    import numpy as np
    return np.ascontiguousarray(a.reshape(-1, P).T)


def build(nc, x, roles, codes, cb2, wqT, wkT, wvT, wp, w_packed, rows_packed,
          units_a, units_b, units_c, bias_cols, out):
    def scratch(name, shape):
        return nc.dram_tensor(name, shape, F32, kind="Internal").ap()

    fold_m = scratch("fold_m", (P, KD * D))
    fold_v = scratch("fold_v", (P, KD * D))
    x1 = scratch("x1", (NROWS + NG * P, GT * D))
    x2 = scratch("x2", (NROWS, GT * D))
    mid = scratch("mid", (3 * NG * P, GT * D))
    with ExitStack() as ctx:
        def sb(name, shape, dt=F32):
            return ctx.enter_context(nc.sbuf_tensor(name, shape, dt))

        consts = (sb("tab_src", [P, 2 * NG], I32), sb("tab_dst", [P, 2 * NG], I32), sb("tab_row", [1, 3 * NG], I32),
                  sb("target_bias", [P, KD, NSEQ]), sb("ident", [P, P]))
        route(nc, consts, roles, codes, cb2)

        w_raw = [sb(f"w_raw{i}", [P, WROW]) for i in range(2)]
        place = (nc.sbuf_base + 31) // 32 * 32
        places = {"o_hi": place, "o_lo": place + 8 * KD * D, "first_c": place + 16 * KD * D}
        factors = [nc.alloc_sbuf_tensor_at(f"factor{i}", [P, KD * D], F32, offset=place + 4 * KD * D * i) for i in range(4)]
        first_c = nc.alloc_sbuf_tensor_at("first_c", [P, KD * D], F32, offset=places["first_c"])
        sb("places", [P, 5 * KD * D + 8])
        raw_in = [ctx.enter_context(nc.semaphore(f"raw_in{i}")) for i in range(2)]
        fold_in = [ctx.enter_context(nc.semaphore(f"fold_in{i}")) for i in range(2)]
        loads = [(factors[i][:].rearrange("p (k n) -> p k n", k=KD), w.rearrange("(k p) n -> p k n", p=P), fold_in[i // 2])
                 for i, w in enumerate((wqT, wkT, wvT, wp))]
        loads.append((first_c[:], units_c[0], raw_in[1]))
        ffn_layers(nc, "first", consts, (0,), x, None, x1, w_packed, rows_packed, w_raw,
                   fold=(loads, ((factors[0], factors[1]), (factors[2], factors[3])), fold_in, raw_in))
        core_layer(nc, consts, (w_raw, first_c, places, raw_in), units_a, units_b, units_c, fold_m, fold_v, bias_cols,
                   x1.rearrange("a (t n) -> (a t) n", n=D), x2.rearrange("a (t n) -> (a t) n", n=D))
        ffn_layers(nc, "last", consts, (1, 2), x2, mid, out, w_packed, rows_packed, w_raw)


def kernel(x, itok_B_1_2, itok_B_17_1546, _lenS,
           L0_cond_W_down, L0_cond_b_down, L0_cond_W_up, L0_cond_b_up, L0_cond_gamma, L0_cond_beta,
           L1_cond_Wq, L1_cond_Wk, L1_cond_Wv, L1_cond_Wp, L1_cond_bp, L1_cond_cW1, L1_cond_cb1,
           L1_cond_cW2, L1_cond_cb2, L1_cond_mW1, L1_cond_mb1, L1_cond_mW2, L1_cond_mb2,
           L2_cond_W_down, L2_cond_b_down, L2_cond_W_up, L2_cond_b_up, L2_cond_gamma, L2_cond_beta,
           L3_cond_W_down, L3_cond_b_down, L3_cond_W_up, L3_cond_b_up, L3_cond_ln_w, L3_cond_ln_b):
    import numpy as np
    import concourse.bacc as bacc
    from concourse.bass_utils import run_bass_kernel_spmd

    def both(*arrays):
        return np.concatenate([np.asarray(a) for a in arrays])

    w_down = both(L0_cond_W_down, L2_cond_W_down, L3_cond_W_down)
    w_up = both(L0_cond_W_up, L2_cond_W_up, L3_cond_W_up)
    b_down = both(L0_cond_b_down, L2_cond_b_down, L3_cond_b_down)
    b_up = both(L0_cond_b_up, L2_cond_b_up, L3_cond_b_up)
    gamma = both(L0_cond_gamma, L2_cond_gamma, L3_cond_ln_w)
    beta = both(L0_cond_beta, L2_cond_beta, L3_cond_ln_b)
    w_packed = np.concatenate([packed_linear(w_down), packed_linear(w_up),
                               np.stack([column_tiles(b) for b in b_down])], axis=-1)
    cw1, cw2, mw1, mw2 = (np.asarray(a) for a in (L1_cond_cW1, L1_cond_cW2, L1_cond_mW1, L1_cond_mW2))
    chunks = [slice(c * D, (c + 1) * D) for c in range(CH)]
    host = {
        "x": np.asarray(x).reshape(NROWS, GT * D),
        "roles": np.asarray(itok_B_1_2).reshape(NSEQ, 1),
        "codes": np.asarray(itok_B_17_1546).reshape(1, NSEQ),
        "cb2": column_tiles(np.asarray(L1_cond_cb2)),
        "wqT": np.asarray(L1_cond_Wq).T, "wkT": np.asarray(L1_cond_Wk).T,
        "wvT": np.asarray(L1_cond_Wv).T, "wp": np.asarray(L1_cond_Wp),
        "w_packed": w_packed,
        "rows_packed": np.stack([b_up, gamma, beta], axis=1),
        "units_a": packed_linear(np.stack([cw1[:, c] for c in chunks] + [mw1[:D, c] for c in chunks])),
        "units_b": packed_linear(np.stack([cw2[c] for c in chunks] + [mw2[c] for c in chunks])),
        "units_c": packed_linear(np.stack([mw1[D:, c] for c in chunks])),
        "bias_cols": np.concatenate([column_tiles(np.asarray(a)) for a in
                                     (L1_cond_cb1, L1_cond_mb1, L1_cond_bp, L1_cond_mb2)], axis=1),
    }
    nc = bacc.Bacc("TRN2", target_bir_lowering=False, num_devices=1)
    arrays, args = {}, {}
    for name, a in host.items():
        arrays[f"in_{name}"] = np.ascontiguousarray(a)
        args[name] = nc.dram_tensor(f"in_{name}", a.shape, mybir.dt.from_np(a.dtype), kind="ExternalInput").ap()
    out = nc.dram_tensor("out_rows", (NROWS + NG * P, GT * D), F32, kind="ExternalOutput").ap()
    build(nc, **args, out=out)
    r = run_bass_kernel_spmd(nc, [arrays], core_ids=[0])
    return r.results[0]["out_rows"][:NROWS].reshape(NSEQ, LEN, D)
```
